# Optimizing a Trainium2 kernel written in Bass

```python
import numpy as np
import jax
import jax.numpy as jnp

def _softmax(x, axis=-1):
    return jax.nn.softmax(x, axis=axis)

def _gelu(x):
    return jax.nn.gelu(x, approximate=True)

def _silu(x):
    return jax.nn.silu(x)

def _sigmoid(x):
    return jax.nn.sigmoid(x)

def _layernorm(x, axis=-1, eps=1e-05):
    m = jnp.mean(x, axis=axis, keepdims=True)
    v = jnp.var(x, axis=axis, keepdims=True)
    return (x - m) / jnp.sqrt(v + eps)

def _scatter_add(tgt, idx, src, axis=0):
    return tgt.at[idx].add(src)

def _segment_sum(src, seg, n):
    return jax.ops.segment_sum(src, seg, n)
kernel_name = 'mk_xattn_ffn_d1_seqx_r4_040e11'

def setup_inputs(seed: int=0):
    np.random.seed(seed)
    _w = jnp.asarray

    def _rec_inputs():
        import jax
        import jax.numpy as jnp
        _rk = jax.random.key(seed)
        x = -0.0002928 + 1 * jax.random.normal(jax.random.fold_in(_rk, 1), (128, 128, 256), jnp.float32)
        _lenS = 128 - jax.random.randint(jax.random.fold_in(_rk, 7), (128,), 0, max(1, 128 // 4) + 1, jnp.int32)
        _lenS2 = 128 - jax.random.randint(jax.random.fold_in(_rk, 8), (128,), 0, max(1, 128 // 4) + 1, jnp.int32)
        _ctx_1024P = jax.random.normal(jax.random.fold_in(_rk, 11), (128, 16, 256), jnp.float32)
        _ctx_1024c = jax.random.dirichlet(jax.random.fold_in(_rk, 511), 0.3 * jnp.ones((16,), jnp.float32), (128, 128))
        _ctx_1024t = jnp.einsum('bsk,bkd->bsd', _ctx_1024c, _ctx_1024P)
        _ctx_1024t = _ctx_1024t * jax.lax.rsqrt(jnp.mean(jnp.square(_ctx_1024t)) + 1e-12) * 0.953939
        ctx_1024 = 4.13588e-05 + 0.999923 * (_ctx_1024t + 0.3 * jax.random.normal(jax.random.fold_in(_rk, 611), (128, 128, 256), jnp.float32))
        return (x, ctx_1024)
    x, ctx_1024 = _rec_inputs()

    def _L0_xattn_setup():
        import jax, jax.numpy as jnp
        import numpy as np
        HIDDEN = 256
        NUM_HEADS = 16
        HEAD_DIM = HIDDEN // NUM_HEADS
        SCALE = 1.0 / float(np.sqrt(HEAD_DIM))
        key = jax.random.key(seed)
        ks = jax.random.split(key, 10)
        B, SQ, SKV = (2, 512, 1024)
        init = 0.02
        return {'query_states': jax.random.normal(ks[0], (B, SQ, HIDDEN), dtype=jnp.float32), 'key_value_states': jax.random.normal(ks[1], (B, SKV, HIDDEN), dtype=jnp.float32), 'Wq': jax.random.normal(ks[2], (HIDDEN, HIDDEN), dtype=jnp.float32) * init, 'bq': jnp.zeros((HIDDEN,), dtype=jnp.float32), 'Wk': jax.random.normal(ks[3], (HIDDEN, HIDDEN), dtype=jnp.float32) * init, 'bk': jnp.zeros((HIDDEN,), dtype=jnp.float32), 'Wv': jax.random.normal(ks[4], (HIDDEN, HIDDEN), dtype=jnp.float32) * init, 'bv': jnp.zeros((HIDDEN,), dtype=jnp.float32), 'Wo': jax.random.normal(ks[5], (HIDDEN, HIDDEN), dtype=jnp.float32) * init, 'bo': jnp.zeros((HIDDEN,), dtype=jnp.float32)}
    _L0_xattn_all = _L0_xattn_setup()
    _L0_xattn_in = {k: v for k, v in _L0_xattn_all.items() if k in ('Wq', 'bq', 'Wk', 'bk', 'Wv', 'bv', 'Wo', 'bo')}
    del _L0_xattn_all

    def _L0_ffn_setup():
        import jax, jax.numpy as jnp
        import numpy as np
        B, K, D = (128, 32, 256)
        E = 32
        H = int(D * 0.25)

        def _rsqrt_uniform(key, shape, d):
            bound = d ** (-0.5)
            return jax.random.uniform(key, shape, jnp.float32, -bound, bound)
        key = jax.random.key(seed)
        ks = jax.random.split(key, 7)
        return {'x': jax.random.normal(ks[0], (B, K, D), jnp.float32), 'router_w': _rsqrt_uniform(ks[1], (E, D), D), 'router_b': _rsqrt_uniform(ks[2], (E,), D), 'weights1': _rsqrt_uniform(ks[3], (E, D, H), H), 'bias1': _rsqrt_uniform(ks[4], (E, H), H), 'weights2': _rsqrt_uniform(ks[5], (E, H, D), D), 'bias2': _rsqrt_uniform(ks[6], (E, D), D)}
    _L0_ffn_all = _L0_ffn_setup()
    _L0_ffn_in = {k: v for k, v in _L0_ffn_all.items() if k in ('router_w', 'router_b', 'weights1', 'bias1', 'weights2', 'bias2')}
    del _L0_ffn_all
    return {'x': x, 'ctx_1024': ctx_1024, 'L0_xattn_Wq': _L0_xattn_in['Wq'], 'L0_xattn_bq': _L0_xattn_in['bq'], 'L0_xattn_Wk': _L0_xattn_in['Wk'], 'L0_xattn_bk': _L0_xattn_in['bk'], 'L0_xattn_Wv': _L0_xattn_in['Wv'], 'L0_xattn_bv': _L0_xattn_in['bv'], 'L0_xattn_Wo': _L0_xattn_in['Wo'], 'L0_xattn_bo': _L0_xattn_in['bo'], 'L0_ffn_router_w': _L0_ffn_in['router_w'], 'L0_ffn_router_b': _L0_ffn_in['router_b'], 'L0_ffn_weights1': _L0_ffn_in['weights1'], 'L0_ffn_bias1': _L0_ffn_in['bias1'], 'L0_ffn_weights2': _L0_ffn_in['weights2'], 'L0_ffn_bias2': _L0_ffn_in['bias2']}

def reference(x, ctx_1024, L0_xattn_Wq, L0_xattn_bq, L0_xattn_Wk, L0_xattn_bk, L0_xattn_Wv, L0_xattn_bv, L0_xattn_Wo, L0_xattn_bo, L0_ffn_router_w, L0_ffn_router_b, L0_ffn_weights1, L0_ffn_bias1, L0_ffn_weights2, L0_ffn_bias2):
    import jax
    import jax.numpy as jnp

    def _L0_xattn_ref(query_states, key_value_states, Wq, bq, Wk, bk, Wv, bv, Wo, bo):
        import jax, jax.numpy as jnp
        import numpy as np
        HIDDEN = 256
        NUM_HEADS = 16
        HEAD_DIM = HIDDEN // NUM_HEADS
        SCALE = 1.0 / float(np.sqrt(HEAD_DIM))
        B, SQ, _ = query_states.shape
        _, SKV, _ = key_value_states.shape
        q = query_states @ Wq.T + bq
        k = key_value_states @ Wk.T + bk
        v = key_value_states @ Wv.T + bv
        q = q.reshape(B, SQ, NUM_HEADS, HEAD_DIM).transpose(0, 2, 1, 3) * SCALE
        k = k.reshape(B, SKV, NUM_HEADS, HEAD_DIM).transpose(0, 2, 1, 3)
        v = v.reshape(B, SKV, NUM_HEADS, HEAD_DIM).transpose(0, 2, 1, 3)
        scores = jnp.einsum('bhqd,bhkd->bhqk', q, k)
        attn = jax.nn.softmax(scores, axis=-1)
        ctx = jnp.einsum('bhqk,bhkd->bhqd', attn, v)
        ctx = ctx.transpose(0, 2, 1, 3).reshape(B, SQ, HIDDEN)
        return ctx @ Wo.T + bo

    def _L0_ffn_ref(x, router_w, router_b, weights1, bias1, weights2, bias2):
        import jax, jax.numpy as jnp
        import numpy as np
        B, K, D = (128, 32, 256)
        E = 32
        H = int(D * 0.25)

        def _rsqrt_uniform(key, shape, d):
            bound = d ** (-0.5)
            return jax.random.uniform(key, shape, jnp.float32, -bound, bound)
        b, k, d = x.shape
        x_flat = x.reshape(-1, d)
        n = x_flat.shape[0]
        logits = x_flat @ router_w.T + router_b
        routed_idx = jnp.argmax(logits, axis=-1)

        def expert_mlp(w1, b1, w2, b2):
            h = jax.nn.relu(x_flat @ w1 + b1)
            return jax.nn.relu(h @ w2 + b2)
        y_all = jax.vmap(expert_mlp)(weights1, bias1, weights2, bias2)
        out_flat = y_all[routed_idx, jnp.arange(n)]
        return out_flat.reshape(b, k, d)
    x = x + _L0_xattn_ref(_layernorm(x, axis=-1), ctx_1024, L0_xattn_Wq, L0_xattn_bq, L0_xattn_Wk, L0_xattn_bk, L0_xattn_Wv, L0_xattn_bv, L0_xattn_Wo, L0_xattn_bo)
    x = x + _L0_ffn_ref(_layernorm(x, axis=-1), L0_ffn_router_w, L0_ffn_router_b, L0_ffn_weights1, L0_ffn_bias1, L0_ffn_weights2, L0_ffn_bias2)
    return x

_drawn_inputs = setup_inputs


def setup_inputs(seed=0):
    import zlib

    import numpy as np

    out = dict(_drawn_inputs(seed))
    spreads = {'L0_xattn_bq': (0.0, 0.8),
     'L0_xattn_bk': (0.0, 0.8),
     'L0_xattn_bv': (0.0, 0.1),
     'L0_xattn_bo': (0.0, 0.1)}
    factors = {'L0_xattn_Wq': 6.776, 'L0_xattn_Wk': 6.384, 'L0_ffn_bias1': 5.772}
    for name, (base, spread) in spreads.items():
        noise = np.random.default_rng([zlib.crc32(name.encode()), seed]).standard_normal(out[name].shape)
        drawn = base * np.exp(spread * noise) if base else spread * noise
        out[name] = jnp.asarray(drawn.astype(out[name].dtype))
    for name, factor in factors.items():
        out[name] = (out[name] * factor).astype(out[name].dtype)
    return out
```

```python
from contextlib import ExitStack

import numpy as np

import concourse.bass as bass
from concourse import mybir

F32 = mybir.dt.float32
BF16 = mybir.dt.bfloat16
I32 = mybir.dt.int32
U32 = mybir.dt.uint32
ALU = mybir.AluOpType
ACT = mybir.ActivationFunctionType
AX = mybir.AxisListType

P = 128
QB = 4
ROW = 260
COL_TOKEN, COL_EXPERT, COL_MEAN, COL_RSTD = 256, 257, 258, 259
NOWHERE = 1 << 30
EPS = 1e-5
PG = 4
ROUND = 1.5 * 2.0 ** 23

C_IDENT, C_TRI, C_SEL, C_ONES, C_MASK, C_IOTA, C_TOKEN = 0, 128, 256, 512, 576, 578, 610
C_ALL = 614


def constants():
    c = np.zeros((P, C_ALL), np.float32)
    p = np.arange(P)
    c[:, C_IDENT:C_IDENT + P] = np.eye(P)
    c[:, C_TRI:C_TRI + P] = p[:, None] < p[None, :]
    for m in range(2):
        c[:, C_SEL + P * m:C_SEL + P * (m + 1)] = -1.0 * (p % 32 == m)[:, None]
        c[:, C_ONES + 32 * m + 16 * m:C_ONES + 32 * m + 16 * m + 16] = 1.0
        c[:, C_MASK + m] = 0.25 * (p % 32 // 16 == m)
    c[:, C_IOTA:C_IOTA + 32] = np.arange(32)
    c[:, C_TOKEN:C_TOKEN + QB] = p[:, None] + P * np.arange(QB)
    return c


def build(nc, x, ctxT, wq, wk, wv, wo, bq, bk, bv, bo, wr, rb, w1, w2, consts, out):
    NB = x.shape[0]
    D = x.shape[2]
    NQ = NB // QB
    E = wr.shape[2]
    HID = w2.shape[1] - 1
    TOKENS = NB * P
    PAGES = -(-(TOKENS // P + E) // PG) * PG
    x_q = x.rearrange("(q b) t d -> q t b d", b=QB)
    out_rows = out.rearrange("b t d -> (b t) d")
    pages = nc.dram_tensor("pages", (PAGES * P, ROW), F32).ap()
    page_view = pages.rearrange("(n p) c -> p n c", p=P)

    ctx = ExitStack()
    with ctx:
        def sb(name, shape, dt=F32):
            return ctx.enter_context(nc.sbuf_tensor(name, [P] + shape, dt))

        def ps(name):
            return ctx.enter_context(nc.psum_tensor(name, [P, 512], F32))

        def sem(name):
            return ctx.enter_context(nc.semaphore(name))

        cst = sb("cst", [C_ALL])
        wq_s, wk_s, wv_s, wo_s = (sb(n, [2, D]) for n in ("wq_s", "wk_s", "wv_s", "wo_s"))
        wr_s = sb("wr_s", [2, P])
        bq_s, bk_s = sb("bq_s", [2]), sb("bk_s", [2])
        bqm = sb("bqm", [2, 2])
        bv_s, bo_s = sb("bv_s", [D]), sb("bo_s", [D])
        rb_s = sb("rb_s", [E])
        ident_b, tri_b, ones_b = sb("ident_b", [P], BF16), sb("tri_b", [P], BF16), sb("ones_b", [P], BF16)
        sel_b = sb("sel_b", [2, P], BF16)
        half = sb("half", [QB])
        xs = sb("xs", [2, QB, D])
        xb = sb("xb", [2, QB, D])
        xn = sb("xn", [QB, D])
        xnT = sb("xnT", [2, QB * P])
        cT = sb("cT", [2, 2, QB * P])
        qT = sb("qT", [2, 2, 2, QB * P])
        qTb = sb("qTb", [2, 2, 2, QB * P], BF16)
        kT = sb("kT", [2, 2, QB * P])
        kTb = sb("kTb", [2, 2, QB * P], BF16)
        vs = sb("vs", [2, QB, 8, 4, 16])
        mx = sb("mx", [2, 2, 4, 32], BF16)
        mxT = sb("mxT", [2, 2 * P], BF16)
        pt = sb("pt", [2, 4, 512])
        rz = sb("rz", [2 * P])
        aT = sb("aT", [2, 2, P])
        row = sb("row", [2, QB, ROW])
        st1, ag1, rs1 = sb("st1", [QB, 6]), sb("ag1", [QB, 2]), sb("rs1", [QB])
        st2 = sb("st2", [QB, 6])
        xn2 = sb("xn2", [QB, D])
        xn2T = sb("xn2T", [2, QB * P])
        lg = sb("lg", [QB, E])
        top, topi, idxf = sb("top", [QB, 8]), sb("topi", [QB, 8], U32), sb("idxf", [QB])
        hot = sb("hot", [2, QB, E], BF16)
        seen = sb("seen", [E], BF16)
        rk = sb("rk", [QB + 1, E])
        B = sb("B", [E])
        Doff = sb("Doff", [E])
        T0 = sb("T0", [1])
        fresh, run, noff, dd = sb("fresh", [E]), sb("run", [E]), sb("noff", [E]), sb("dd", [E])
        zer = sb("zer", [E])
        t1, t2 = sb("t1", [QB, E]), sb("t2", [QB, E])
        grew, shift = sb("grew", [E]), sb("shift", [E])
        slot = sb("slot", [QB])
        slot_i = sb("slot_i", [2, QB], U32)
        tok = sb("tok", [QB])
        tsum = sb("tsum", [E])
        empty = sb("empty", [ROW])
        table = ctx.enter_context(nc.sbuf_tensor("table", [1, PAGES], I32))
        pr = sb("pr", [PG, ROW])
        w1s = sb("w1s", [PG, 2 * HID + 1])
        w2s = ctx.enter_context(nc.sbuf_tensor("w2s", [HID + 1, PG, D], F32))
        pn = sb("pn", [PG, D])
        pnT = sb("pnT", [2, 2 * P])
        hT = ctx.enter_context(nc.sbuf_tensor("hT", [HID + 1, 2, P], F32))
        po = sb("po", [PG, D])

        sc = [ps(f"sc{j}") for j in range(4)]
        b4, b5, b6, b7 = ps("b4"), ps("b5"), ps("b6"), ps("b7")
        b5h = b5[:, :].bitcast(BF16)

        names = """ld_w ld_w2 fill ld_x0 ld_x1 ld_c0 ld_c1 table_in page_in0 page_in1 page_in2 page_in3 scattered wrote0 wrote1 wrote2 wrote3
          cst_ready pool_init dve_init
          S_done xnT_done proj_done V_done mxT_done PV_done T_done O_done xn2T_done lg_done rk_done
          xnT_out proj_out exp_out xn2T_out
          max_out V_out lg_out mxT_out inv_out aT_out x2_out stat2_out agg2_out xn2_out
          stat1_out agg1_out xn_out top_out topi_out idx_out hot_out rk_out tsum_out seen_out
          need_out need_frac need_round pages_run pages_first fresh_start fresh_shift
          in_fresh old_slot fresh_step slot_each slot_own slot_sum page_total grew_out B_out shift_out D_out slot_out tok_next
          var2_out rstd2_out var1_out rstd1_out xb_out cast_out tok_out
          pn_out pT_done h_done y_done pT_out h_out po_out""".split()
        S = {n: sem(n) for n in names}

        def after(eng, name, per, q, k):
            eng.wait_ge(S[name], q * per + (k + 1))

        def apart(eng, *waits):
            waits = [(S[name], value if isinstance(value, int) else eng.to_reg(value)) for name, value in waits]
            eng.wait_ge(*settled[eng.engine])
            for semaphore, value in waits:
                eng.wait_ge(semaphore, value)

        def arrived(eng, name, q, par):
            eng.wait_ge(S[f"{name}{par}"], (q - par) * 8 + 16)

        ET = mybir.EngineType
        settled = {ET.DVE: (S["dve_init"], 6), ET.Pool: (S["pool_init"], 7), ET.SP: (S["pool_init"], 6)}

        block = ctx.enter_context(nc.Block())
        LO, HI = 2, NQ - 2

        def slots(eng, step):
            for s in range(LO):
                step(s, s % 2, s)
            with eng.Fori(0, (HI - LO) // 2) as i:
                for k in range(2):
                    step(i * 2 + (LO + k), k, LO)
            for s in range(HI, NQ + 2):
                step(s, s % 2, s)

        def has(at, lead):
            return 0 <= at + lead < NQ

        @block.sync
        def _(sp):
            for dst, src in ((cst[:, :], consts), (wk_s[:, :, :], wk), (wv_s[:, :, :], wv),
                             (wq_s[:, :, :], wq), (bq_s[:, :], bq), (bk_s[:, :], bk), (bv_s[:, :], bv)):
                sp.dma_start(dst, src).then_inc(S["ld_w"], 16)

            def load(q, par, at):
                if at >= 2:
                    apart(sp, ("xn_out", q * 4 - 4), ("xb_out", q - 1))
                sp.dma_start(xs[:, par], x_q[bass.ds(q, 1)].rearrange("a t b d -> t (a b) d")).then_inc(S[f"ld_x{par}"], 16)
                if at >= 2:
                    apart(sp, ("proj_done", q * 4 - 6), ("V_done", q * 4 - 4))
                sp.dma_start(cT[:, par], ctxT[bass.ds(q, 1)].rearrange("a p c t -> p (a c) t")).then_inc(S[f"ld_c{par}"], 16)

            load(0, 0, 0)
            for dst, src in ((wo_s[:, :, :], wo), (bo_s[:, :], bo), (rb_s[:, :], rb)):
                sp.dma_start(dst, src).then_inc(S["ld_w2"], 16)
            sp.wait_ge(S["pool_init"], 6)
            sp.dma_start(wr_s[:, :, 0:E], wr).then_inc(S["ld_w2"], 16)
            load(1, 1, 1)
            with sp.Fori(0, (NQ - 2) // 2) as i:
                for k in range(2):
                    load(i * 2 + (2 + k), k, 2)

            sp.wait_ge(S["scattered"], 64 * NQ)
            with nc.allow_non_contiguous_dma(reason="one word of each page"):
                sp.dma_start(table[0:1, :], pages.rearrange("(n p) c -> n p c", p=P)[:, 0, COL_EXPERT:COL_EXPERT + 1]
                             .rearrange("n c -> c n").bitcast(I32)).then_inc(S["table_in"], 16)
            sp.wait_ge(S["table_in"], 16)

            def load_page(n, r, first):
                e = sp.value_load(table[0:1, bass.ds(n, 1)], min_val=0, max_val=E - 1)
                if not first:
                    apart(sp, ("po_out", n - PG + 1), (f"wrote{r}", (n - r) * (16 // PG)))
                sp.dma_start(pr[:, r, :], page_view[:, bass.ds(n, 1), :].rearrange("p n c -> p (n c)")).then_inc(S[f"page_in{r}"], 16)
                sp.dma_start(w1s[:, r, :], w1[bass.ds(e, 1)].rearrange("e p c -> p (e c)")).then_inc(S[f"page_in{r}"], 16)
                sp.dma_start(w2s[:, r, :], w2[bass.ds(e, 1)].rearrange("e p c -> p (e c)")).then_inc(S[f"page_in{r}"], 16)

            for n in range(2 * PG):
                load_page(n, n % PG, n < PG)
            with sp.Fori(2, PAGES // PG) as i:
                for r in range(PG):
                    load_page(i * PG + r, r, False)
            for r in range(PG):
                sp.wait_ge(S[f"wrote{r}"], 16 * (PAGES // PG))

        @block.gpsimd
        def _(pool):
            pool.memset(empty[:, :], 0.0).then_inc(S["pool_init"], 1)
            pool.memset(vs[:, :, :, :, :, :], 0.0).then_inc(S["pool_init"], 1)
            pool.memset(mx[:, :, :, :, :], 0.0).then_inc(S["pool_init"], 1)
            pool.memset(seen[:, :], 0.0).then_inc(S["pool_init"], 1)
            pool.memset(half[:, :], -0.5).then_inc(S["pool_init"], 1)
            pool.memset(wr_s[:, :, :], 0.0).then_inc(S["pool_init"], 1)
            pool.wait_ge(S["pool_init"], 6)
            pool.memset(empty[:, COL_TOKEN:COL_TOKEN + 1].bitcast(I32), NOWHERE).then_inc(S["pool_init"], 1)
            pool.wait_ge(S["pool_init"], 7)
            NF = 8
            for f in range(NF):
                n = PAGES // NF
                pool.dma_start(page_view[:, n * f:n * (f + 1), :],
                               empty[:, :].unsqueeze(1).to_broadcast([P, n, ROW])).then_inc(S["fill"], 16)

            last_slot, last_token = pool.to_reg(PAGES * P - 1), pool.to_reg(TOKENS - 1)

            def rstd1(q):
                apart(pool, ("agg1_out", q * 4 + 4))
                pool.tensor_scalar(rs1[:, :], ag1[:, :, 1], EPS, None, ALU.add).then_inc(S["var1_out"], 1)
                after(pool, "var1_out", 1, q, 0)
                pool.tensor_tensor(rs1[:, :], rs1[:, :], half[:, :], ALU.pow).then_inc(S["rstd1_out"], 1)

            def rstd2(q, par):
                apart(pool, ("agg2_out", q * 4 + 4))
                v = row[:, par, :, COL_RSTD]
                pool.tensor_scalar(v, v, EPS, None, ALU.add).then_inc(S["var2_out"], 1)
                after(pool, "var2_out", 1, q, 0)
                pool.tensor_tensor(v, v, half[:, :], ALU.pow).then_inc(S["rstd2_out"], 1)

            def add_bo(q, par, at):
                if at == 0:
                    pool.wait_ge(S["ld_w2"], 64)
                arrived(pool, "ld_x", q, par)
                if at >= 2:
                    after(pool, "x2_out", 4, q - 2, 3)
                pool.tensor_tensor(xb[:, par], xs[:, par], bo_s[:, :].unsqueeze(1).to_broadcast([P, QB, D]),
                                   ALU.add).then_inc(S["xb_out"], 1)

            def cast(q, par, k, at):
                apart(pool, ("proj_out", q * 4 + (k + 1)), *([("S_done", q * 4 - 4)] if at >= 2 else []))
                if k < 2:
                    pool.tensor_copy(kTb[:, par, k], kT[:, par, k]).then_inc(S["cast_out"], 1)
                else:
                    pool.tensor_copy(qTb[:, par, k - 2], qT[:, par, k - 2]).then_inc(S["cast_out"], 1)

            def scatter(q, par, at):
                if at == 0:
                    pool.wait_ge(S["fill"], 16 * NF)
                apart(pool, ("slot_out", q + 1))
                for u in range(QB):
                    pool.indirect_dma_start(
                        pages, bass.IndirectOffsetOnAxis(slot_i[:, par, u:u + 1], 0), row[:, par, u, :], None,
                        bounds_check=last_slot, oob_is_err=False).then_inc(S["scattered"], 16)

            rstd1(0)
            add_bo(0, 0, 0)
            for k in range(4):
                cast(0, 0, k, 0)
            rstd1(1)

            def step(s, par, at):
                if has(at, -1):
                    rstd2(s - 1, 1 - par)
                if has(at, 1):
                    cast(s + 1, 1 - par, 0, at + 1)
                if has(at, -2):
                    scatter(s - 2, par, at - 2)
                if has(at, 1):
                    add_bo(s + 1, 1 - par, at + 1)
                    cast(s + 1, 1 - par, 1, at + 1)
                    cast(s + 1, 1 - par, 2, at + 1)
                if has(at, 2):
                    rstd1(s + 2)
                if has(at, 1):
                    cast(s + 1, 1 - par, 3, at + 1)

            slots(pool, step)

            def write_page(n, r):
                apart(pool, ("po_out", n + 1))
                pool.indirect_dma_start(
                    out_rows, bass.IndirectOffsetOnAxis(pr[:, r, COL_TOKEN:COL_TOKEN + 1].bitcast(U32), 0),
                    po[:, r, :], None, bounds_check=last_token, oob_is_err=False).then_inc(S[f"wrote{r}"], 16)

            with pool.Fori(0, PAGES // PG) as i:
                for r in range(PG):
                    write_page(i * PG + r, r)

        @block.scalar
        def _(act):
            act.wait_ge(S["cst_ready"], 5)

            def xnT_copy(q, h, at):
                after(act, "xnT_done", 2, q, h)
                if at >= 1:
                    after(act, "proj_done", 4, q - 1, 3)
                src = b5[:, :].rearrange("p (u c t) -> p c u t", u=2, c=2)
                dst = xnT[:, :, 2 * P * h:2 * P * (h + 1)].rearrange("p c (u t) -> p c u t", u=2)
                for c in range(2):
                    ins = act.activation(dst[:, c], src[:, c], ACT.Copy)
                ins.then_inc(S["xnT_out"], 1)

            def proj_copy(q, par, k, at):
                after(act, "proj_done", 4, q, k)
                if at >= 2:
                    after(act, "T_done", 16, q - 2, 15)
                    after(act, "cast_out", 4, q - 2, 3)
                if k < 2:
                    act.activation(kT[:, par, k], b4[:, :], ACT.Identity, bias=bk_s[:, k:k + 1]).then_inc(S["proj_out"], 1)
                else:
                    c = k - 2
                    act.activation(qT[:, par, c, 0], b4[:, :], ACT.Identity, bias=bqm[:, c, 0:1], scale=cst[:, C_MASK:C_MASK + 1])
                    act.activation(qT[:, par, c, 1], b4[:, :], ACT.Identity, bias=bqm[:, c, 1:2],
                                   scale=cst[:, C_MASK + 1:C_MASK + 2]).then_inc(S["proj_out"], 1)

            def exps(q, u, at):
                for j in range(4):
                    after(act, "T_done", 16, q, 4 * u + j)
                    if j == 0 and (at >= 1 or u >= 2):
                        qq, uu = (q, u - 2) if u >= 2 else (q - 1, u + 2)
                        after(act, "PV_done", 4, qq, uu)
                    act.activation(pt[:, u % 2, j], sc[j][:, :], ACT.Exp).then_inc(S["exp_out"], 1)

            def xn2T_copy(q, h, at):
                after(act, "xn2T_done", 2, q, h)
                if at >= 1:
                    after(act, "lg_done", 1, q - 1, 0)
                src = b5[:, :].rearrange("p (u c t) -> p c u t", u=2, c=2)
                dst = xn2T[:, :, 2 * P * h:2 * P * (h + 1)].rearrange("p c (u t) -> p c u t", u=2)
                for c in range(2):
                    ins = act.activation(dst[:, c], src[:, c], ACT.Copy)
                ins.then_inc(S["xn2T_out"], 1)

            xnT_copy(0, 0, 0)
            xnT_copy(0, 1, 0)
            for k in range(4):
                proj_copy(0, 0, k, 0)

            def step(s, par, at):
                for u in range(QB):
                    if has(at, 1):
                        if u < 2:
                            xnT_copy(s + 1, u, at + 1)
                        proj_copy(s + 1, 1 - par, u, at + 1)
                    if has(at, 0):
                        exps(s, u, at)
                    if has(at, -1) and u in (1, 2):
                        xn2T_copy(s - 1, u - 1, at - 1)

            slots(act, step)

            def pnT_copy(n, r, first):
                after(act, "pT_done", 1, n, 0)
                if not first:
                    after(act, "h_done", 1, n - 2, 0)
                act.activation(pnT[:, r % 2, :], b4[:, 0:256] if r % 2 == 0 else b5[:, 0:256], ACT.Copy).then_inc(S["pT_out"], 1)

            def h_copy(n, r, first):
                after(act, "h_done", 1, n, 0)
                if not first:
                    after(act, "y_done", 1, n - 2, 0)
                act.activation(hT[0:HID, r % 2, :], b6[0:HID, 0:P] if r % 2 == 0 else b7[0:HID, 0:P], ACT.Relu,
                               bias=w1s[0:HID, r, 2 * HID:2 * HID + 1]).then_inc(S["h_out"], 1)

            for n in range(2 * PG):
                pnT_copy(n, n % PG, n < 2)
                if n >= 1:
                    h_copy(n - 1, (n - 1) % PG, n - 1 < 2)
            with act.Fori(2, PAGES // PG) as i:
                for r in range(PG):
                    pnT_copy(i * PG + r, r, False)
                    h_copy(i * PG + (r - 1), (r - 1) % PG, False)
            h_copy(PAGES - 1, PG - 1, False)

        @block.vector
        def _(dve):
            dve.wait_ge(S["ld_w"], 16 * 7)
            dve.memset(ones_b[:, :], 1.0).then_inc(S["cst_ready"], 1)
            dve.tensor_copy(ident_b[:, :], cst[:, C_IDENT:C_IDENT + P]).then_inc(S["cst_ready"], 1)
            dve.tensor_copy(tri_b[:, :], cst[:, C_TRI:C_TRI + P]).then_inc(S["cst_ready"], 1)
            dve.tensor_copy(sel_b[:, :, :], cst[:, C_SEL:C_SEL + 2 * P].rearrange("p (m k) -> p m k", m=2)).then_inc(S["cst_ready"], 1)
            for c in range(2):
                ins = dve.tensor_scalar(bqm[:, c, :], cst[:, C_MASK:C_MASK + 2], bq_s[:, c:c + 1], None, ALU.mult)
            ins.then_inc(S["cst_ready"], 1)
            dve.memset(B[:, :], 0.0).then_inc(S["dve_init"], 1)
            dve.memset(Doff[:, :], 0.0).then_inc(S["dve_init"], 1)
            dve.memset(T0[:, :], 0.0).then_inc(S["dve_init"], 1)
            dve.memset(zer[:, :], 0.0).then_inc(S["dve_init"], 1)
            dve.memset(hT[:, :, :], 1.0).then_inc(S["dve_init"], 1)
            dve.tensor_copy(tok[:, :], cst[:, C_TOKEN:C_TOKEN + QB]).then_inc(S["dve_init"], 1)
            dve.wait_ge(S["dve_init"], 6)

            def stats1(q, par):
                arrived(dve, "ld_x", q, par)
                for u in range(QB):
                    dve.bn_stats(st1[:, u, :], xs[:, par, u, :]).then_inc(S["stat1_out"], 1)
                for u in range(QB):
                    apart(dve, ("stat1_out", q * 4 + (u + 1)))
                    dve.bn_aggr(ag1[:, u, :], st1[:, u, :]).then_inc(S["agg1_out"], 1)

            def norm1(q, par, at):
                after(dve, "rstd1_out", 1, q, 0)
                if at >= 1:
                    after(dve, "xnT_done", 2, q - 1, 1)
                for u in range(QB):
                    dve.tensor_scalar(xn[:, u, :], xs[:, par, u, :], ag1[:, u, 0:1], rs1[:, u:u + 1],
                                      ALU.subtract, ALU.mult).then_inc(S["xn_out"], 1)

            def maxima(q, u, at):
                if at >= 1 or u >= 2:
                    qq, uu = (q, u - 2) if u >= 2 else (q - 1, u + 2)
                    after(dve, "mxT_done", 4, qq, uu)
                after(dve, "S_done", 4, q, u)
                for j in range(4):
                    ins = dve.tensor_reduce(mx[:, u % 2, :, j, 0:2], sc[j][:, :].rearrange("p (c m k) -> p c m k", c=2, m=2),
                                            AX.X, ALU.max)
                ins.then_inc(S["max_out"], 1)

            def v_copy(q, par, u, at):
                after(dve, "V_done", 4, q, u)
                if at >= 2:
                    after(dve, "PV_done", 4, q - 2, u)
                for m in range(2):
                    ins = dve.tensor_tensor(
                        vs[:, par, u, :, 3 * m, :], b6[:, 0:D].rearrange("p (g m d) -> p g m d", g=8, m=2)[:, :, m, :],
                        bv_s[:, :].rearrange("p (g m d) -> p g m d", g=8, m=2)[:, :, m, :], ALU.add)
                ins.then_inc(S["V_out"], 1)

            def mxT_copy(q, u, at):
                after(dve, "mxT_done", 4, q, u)
                dve.tensor_copy(mxT[:, u % 2, :], b5h[:, 0:2 * P]).then_inc(S["mxT_out"], 1)

            def attend_copy(q, u, at):
                after(dve, "PV_done", 4, q, u)
                dve.reciprocal(rz[:, :], b7[:, 2 * P:4 * P]).then_inc(S["inv_out"], 1)
                after(dve, "inv_out", 4, q, u)
                if at >= 1 or u >= 2:
                    qq, uu = (q, u - 2) if u >= 2 else (q - 1, u + 2)
                    after(dve, "O_done", 4, qq, uu)
                dve.tensor_tensor(aT[:, u % 2].rearrange("p c t -> p (c t)"), b7[:, 0:2 * P], rz[:, :], ALU.mult).then_inc(S["aT_out"], 1)

            def residual(q, par, u, at):
                after(dve, "O_done", 4, q, u)
                after(dve, "xb_out", 1, q, 0)
                if at >= 2 and u == 0:
                    dve.wait_ge(S["scattered"], (q - 1) * 64)
                dve.tensor_tensor(row[:, par, u, 0:D], b6[:, D:2 * D], xb[:, par, u, :], ALU.add).then_inc(S["x2_out"], 1)
                after(dve, "x2_out", 4, q, u)
                dve.bn_stats(st2[:, u, :], row[:, par, u, 0:D]).then_inc(S["stat2_out"], 1)
                apart(dve, ("stat2_out", q * 4 + (u + 1)))
                dve.bn_aggr(row[:, par, u, COL_MEAN:COL_MEAN + 2], st2[:, u, :]).then_inc(S["agg2_out"], 1)

            def norm2(q, par, at):
                after(dve, "rstd2_out", 1, q, 0)
                if at >= 1:
                    after(dve, "xn2T_done", 2, q - 1, 1)
                for u in range(QB):
                    dve.tensor_scalar(xn2[:, u, :], row[:, par, u, 0:D], row[:, par, u, COL_MEAN:COL_MEAN + 1],
                                      row[:, par, u, COL_RSTD:COL_RSTD + 1], ALU.subtract, ALU.mult).then_inc(S["xn2_out"], 1)

            def logits(q):
                after(dve, "lg_done", 1, q, 0)
                dve.tensor_tensor(lg[:, :, :], b6[:, :].rearrange("p (u k) -> p u k", u=QB)[:, :, 0:E],
                                  rb_s[:, :].unsqueeze(1).to_broadcast([P, QB, E]), ALU.add).then_inc(S["lg_out"], 1)

            def choose(q, par, at):
                apart(dve, ("lg_out", q + 1))
                for u in range(QB):
                    dve.max(top[:, u, :], lg[:, u, :]).then_inc(S["top_out"], 1)
                for u in range(QB):
                    apart(dve, ("top_out", q * 4 + (u + 1)))
                    dve.max_index(topi[:, u, :], top[:, u, :], lg[:, u, :]).then_inc(S["topi_out"], 1)
                after(dve, "topi_out", 4, q, 3)
                dve.tensor_copy(idxf[:, :], topi[:, :, 0]).then_inc(S["idx_out"], 1)
                dve.tensor_copy(row[:, par, :, COL_EXPERT].bitcast(U32), topi[:, :, 0])
                dve.tensor_copy(row[:, par, :, COL_TOKEN].bitcast(I32), tok[:, :]).then_inc(S["tok_out"], 1)
                after(dve, "idx_out", 1, q, 0)
                dve.tensor_tensor(hot[:, par], cst[:, C_IOTA:C_IOTA + E].unsqueeze(1).to_broadcast([P, QB, E]),
                                  idxf[:, :].unsqueeze(2).to_broadcast([P, QB, E]), ALU.is_equal).then_inc(S["hot_out"], 1)
                after(dve, "tok_out", 1, q, 0)
                dve.tensor_scalar(tok[:, :], tok[:, :], float(QB * P), None, ALU.add).then_inc(S["tok_next"], 1)

            def rank_copy(q, par):
                after(dve, "rk_done", 1, q, 0)
                dve.tensor_copy(rk[:, :, :].rearrange("p u e -> p (u e)"), b6[:, 0:(QB + 1) * E]).then_inc(S["rk_out"], 1)
                after(dve, "hot_out", 1, q, 0)
                dve.tensor_reduce(tsum[:, :], hot[:, par].rearrange("p u e -> p e u"), AX.X, ALU.add).then_inc(S["tsum_out"], 1)
                after(dve, "tok_next", 1, q, 0)
                after(dve, "tsum_out", 1, q, 0)
                dve.tensor_tensor(seen[:, :], seen[:, :], tsum[:, :], ALU.add).then_inc(S["seen_out"], 1)
                after(dve, "seen_out", 1, q, 0)

            def place(q, par):
                def own(name, ins):
                    ins.then_inc(S[name], 1)
                    after(dve, name, 1, q, 0)

                def each(t):
                    return t[:, :].unsqueeze(1).to_broadcast([P, QB, E])

                after(dve, "rk_out", 1, q, 0)
                rank, count = rk[:, 0:QB, :], rk[:, QB, :]
                own("need_out", dve.tensor_tensor(fresh[:, :], count, B[:, :], ALU.subtract))
                dve.tensor_tensor(t1[:, :, :], rank, each(B), ALU.is_ge).then_inc(S["in_fresh"], 1)
                own("need_frac", dve.tensor_scalar(fresh[:, :], fresh[:, :], 1.0 / P, (P - 1.0) / (2 * P), ALU.mult, ALU.add))
                dve.tensor_tensor(t2[:, :, :], rank, each(Doff), ALU.add).then_inc(S["old_slot"], 1)
                own("need_round", dve.tensor_scalar(fresh[:, :], fresh[:, :], ROUND, ROUND, ALU.add, ALU.subtract))
                own("pages_run", dve.tensor_tensor_scan(run[:, :], fresh[:, :], zer[:, :], T0[:, 0:1], ALU.add, ALU.add))
                dve.tensor_copy(T0[:, 0:1], run[:, E - 1:E]).then_inc(S["page_total"], 1)
                own("pages_first", dve.tensor_tensor(noff[:, :], run[:, :], fresh[:, :], ALU.subtract))
                own("fresh_start", dve.scalar_tensor_tensor(noff[:, :], noff[:, :], float(P), B[:, :], ALU.mult, ALU.subtract))
                own("fresh_shift", dve.tensor_tensor(dd[:, :], noff[:, :], Doff[:, :], ALU.subtract))
                after(dve, "in_fresh", 1, q, 0)
                own("fresh_step", dve.tensor_tensor(t1[:, :, :], t1[:, :, :], each(dd), ALU.mult))
                after(dve, "old_slot", 1, q, 0)
                own("slot_each", dve.tensor_tensor(t1[:, :, :], t1[:, :, :], t2[:, :, :], ALU.add))
                dve.tensor_scalar(grew[:, :], fresh[:, :], 1.0, None, ALU.min).then_inc(S["grew_out"], 1)
                dve.scalar_tensor_tensor(B[:, :], fresh[:, :], float(P), B[:, :], ALU.mult, ALU.add).then_inc(S["B_out"], 1)
                own("slot_own", dve.tensor_tensor(t1[:, :, :], t1[:, :, :], hot[:, par], ALU.mult))
                after(dve, "grew_out", 1, q, 0)
                dve.tensor_tensor(shift[:, :], grew[:, :], dd[:, :], ALU.mult).then_inc(S["shift_out"], 1)
                own("slot_sum", dve.tensor_reduce(slot[:, :], t1[:, :, :], AX.X, ALU.add))
                dve.tensor_copy(slot_i[:, par, :], slot[:, :]).then_inc(S["slot_out"], 1)
                after(dve, "shift_out", 1, q, 0)
                own("D_out", dve.tensor_tensor(Doff[:, :], Doff[:, :], shift[:, :], ALU.add))
                after(dve, "B_out", 1, q, 0)
                after(dve, "page_total", 1, q, 0)

            stats1(0, 0)
            norm1(0, 0, 0)
            dve.wait_ge(S["pool_init"], 3)
            for u in range(QB):
                v_copy(0, 0, u, 0)
            stats1(1, 1)
            norm1(1, 1, 1)

            def step(s, par, at):
                for u in range(QB):
                    if has(at, 0):
                        maxima(s, u, at)
                    if has(at, 1):
                        v_copy(s + 1, 1 - par, u, at + 1)
                    if has(at, -1) and u == 3:
                        logits(s - 1)
                    if has(at, 0):
                        mxT_copy(s, u, at)
                    if has(at, -1) and u == 1:
                        norm2(s - 1, 1 - par, at - 1)
                    q1, par1, at1, u1 = (s, par, at, u - 1) if u else (s - 1, 1 - par, at - 1, 3)
                    if has(at1, 0):
                        attend_copy(q1, u1, at1)
                        residual(q1, par1, u1, at1)
                    if has(at, -2) and u == 0:
                        place(s - 2, par)
                    if has(at, 2) and u == 2:
                        stats1(s + 2, par)
                    if has(at, 2) and u == 3:
                        norm1(s + 2, par, at + 2)
                    if has(at, -1) and u == 3:
                        choose(s - 1, 1 - par, at - 1)
                        rank_copy(s - 1, 1 - par)

            slots(dve, step)

            def page_norm(n, r, first):
                dve.wait_ge(S[f"page_in{r}"], (n - r) * (48 // PG) + 48)
                if not first:
                    after(dve, "pT_done", 1, n - PG, 0)
                dve.tensor_scalar(pn[:, r, :], pr[:, r, 0:D], pr[:, r, COL_MEAN:COL_MEAN + 1],
                                  pr[:, r, COL_RSTD:COL_RSTD + 1], ALU.subtract, ALU.mult).then_inc(S["pn_out"], 1)

            def page_out(n, r, first):
                after(dve, "y_done", 1, n, 0)
                if not first:
                    dve.wait_ge(S[f"wrote{r}"], (n - r) * (16 // PG))
                dve.scalar_tensor_tensor(po[:, r, :], sc[r % 2][:, 0:D], 0.0, pr[:, r, 0:D], ALU.max, ALU.add).then_inc(S["po_out"], 1)

            for n in range(2 * PG):
                page_norm(n, n % PG, n < PG)
                if n >= 2:
                    page_out(n - 2, (n - 2) % PG, n - 2 < PG)
            with dve.Fori(2, PAGES // PG) as i:
                for r in range(PG):
                    page_norm(i * PG + r, r, False)
                    page_out(i * PG + (r - 2), (r - 2) % PG, False)
            for n in (PAGES - 2, PAGES - 1):
                page_out(n, n % PG, False)

        @block.tensor
        def _(pe):
            ident = cst[:, C_IDENT:C_IDENT + P]
            pe.wait_ge(S["cst_ready"], 5)

            def xn_transpose(q, h, at):
                after(pe, "xn_out", 4, q, 2 * h + 1)
                if h == 1:
                    after(pe, "xnT_out", 2, q, 0)
                for v in range(2):
                    for c in range(2):
                        ins = pe.transpose(b5[:, (2 * v + c) * P:(2 * v + c + 1) * P], xn[:, 2 * h + v, c * P:(c + 1) * P], ident)
                ins.then_inc(S["xnT_done"], 1)

            def project(q, par, k, at):
                c = k % 2
                w, src = (wk_s, cT[:, par]) if k < 2 else (wq_s, xnT)
                if k == 0:
                    arrived(pe, "ld_c", q, par)
                if k == 2:
                    after(pe, "xnT_out", 2, q, 1)
                if k > 0:
                    after(pe, "proj_out", 4, q, k - 1)
                elif at >= 1:
                    after(pe, "proj_out", 4, q - 1, 3)
                for i in range(2):
                    ins = pe.matmul(b4[:, :], w[:, i, c * P:(c + 1) * P], src[:, i, :], start=(i == 0), stop=(i == 1))
                ins.then_inc(S["proj_done"], 1)

            def values(q, par, u):
                if u == 0:
                    arrived(pe, "ld_c", q, par)
                for i in range(2):
                    ins = pe.matmul(b6[:, 0:D], cT[:, par, i, u * P:(u + 1) * P], wv_s[:, i, :], start=(i == 0), stop=(i == 1))
                ins.then_inc(S["V_done"], 1)

            def scores_for_max(q, par, u):
                if u == 0:
                    after(pe, "cast_out", 4, q, 3)
                for c in range(2):
                    for m in range(2):
                        for j in range(4):
                            r = slice(32 * j, 32 * j + 32)
                            ins = pe.matmul(sc[j][:, (2 * c + m) * P:(2 * c + m + 1) * P], qTb[r, par, c, m, u * P:(u + 1) * P],
                                            kTb[r, par, c, u * P:(u + 1) * P], start=True, stop=True)
                ins.then_inc(S["S_done"], 1)

            def max_transpose(q, u):
                after(pe, "max_out", 4, q, u)
                for c in range(2):
                    ins = pe.transpose(b5h[:, c * P:(c + 1) * P], mx[:, u % 2, c].rearrange("p j m -> p (j m)"), ident_b[:, :])
                ins.then_inc(S["mxT_done"], 1)

            def scores(q, par, u):
                for c in range(2):
                    for j in range(4):
                        r = slice(32 * j, 32 * j + 32)
                        pe.matmul(sc[j][:, 2 * c * P:2 * (c + 1) * P], kT[r, par, c, u * P:(u + 1) * P],
                                  qT[r, par, c, :, u * P:(u + 1) * P], start=True, stop=False)
                    if c == 0:
                        after(pe, "mxT_out", 4, q, u)
                    for j in range(4):
                        r = slice(32 * j, 32 * j + 32)
                        for m in range(2):
                            ins = pe.matmul(sc[j][:, (2 * c + m) * P:(2 * c + m + 1) * P], sel_b[r, m, :],
                                            mxT[r, u % 2, c * P:(c + 1) * P], start=False, stop=(m == 1))
                        if c == 1:
                            ins.then_inc(S["T_done"], 1)

            def attend(q, par, u):
                for part in range(2):
                    for c in range(2):
                        for m in range(2):
                            for j in range(4):
                                w = (vs[:, par, u, 4 * c + j].rearrange("p a d -> p (a d)")[:, 32 * m:32 * m + 32] if part == 0
                                     else cst[:, C_ONES + 32 * m:C_ONES + 32 * m + 32])
                                ins = pe.matmul(b7[32 * j:32 * j + 32, (2 * part + c) * P:(2 * part + c + 1) * P], w,
                                                pt[:, u % 2, j, (2 * c + m) * P:(2 * c + m + 1) * P], start=(m == 0), stop=(m == 1))
                ins.then_inc(S["PV_done"], 1)

            def project_out(q, u):
                after(pe, "aT_out", 4, q, u)
                for i in range(2):
                    ins = pe.matmul(b6[:, D:2 * D], aT[:, u % 2, i, :], wo_s[:, i, :], start=(i == 0), stop=(i == 1))
                ins.then_inc(S["O_done"], 1)

            def xn2_transpose(q, h):
                after(pe, "xn2_out", 4, q, 2 * h + 1)
                for v in range(2):
                    for c in range(2):
                        ins = pe.transpose(b5[:, (2 * v + c) * P:(2 * v + c + 1) * P], xn2[:, 2 * h + v, c * P:(c + 1) * P], ident)
                ins.then_inc(S["xn2T_done"], 1)

            def logits(q):
                after(pe, "xn2T_out", 2, q, 1)
                for u in range(QB):
                    for i in range(2):
                        ins = pe.matmul(b6[:, u * P:(u + 1) * P], xn2T[:, i, u * P:(u + 1) * P], wr_s[:, i, :],
                                        start=(i == 0), stop=(i == 1))
                ins.then_inc(S["lg_done"], 1)

            def ranks(q, par, at):
                after(pe, "hot_out", 1, q, 0)
                if at >= 1:
                    after(pe, "seen_out", 1, q - 1, 0)
                pe.matmul(b6[:, 0:QB * E], ones_b[:, :], seen[:, :].unsqueeze(1).to_broadcast([P, QB, E]), start=True, stop=False)
                for v in range(QB - 1):
                    pe.matmul(b6[:, (v + 1) * E:QB * E], ones_b[:, :], hot[:, par, v:v + 1].to_broadcast([P, QB - 1 - v, E]),
                              start=False, stop=False, skip_group_check=True)
                pe.matmul(b6[:, 0:QB * E], tri_b[:, :], hot[:, par], start=False, stop=True)
                pe.matmul(b6[:, QB * E:(QB + 1) * E], ones_b[:, :], seen[:, :], start=True, stop=False)
                for v in range(QB):
                    ins = pe.matmul(b6[:, QB * E:(QB + 1) * E], ones_b[:, :], hot[:, par, v], start=False, stop=(v == QB - 1))
                ins.then_inc(S["rk_done"], 1)

            xn_transpose(0, 0, 0)
            xn_transpose(0, 1, 0)
            for k in range(4):
                project(0, 0, k, 0)
            for u in range(QB):
                if u:
                    after(pe, "V_out", 4, 0, u - 1)
                values(0, 0, u)
            pe.wait_ge(S["ld_w2"], 64)

            def step(s, par, at):
                for u in range(QB):
                    q1, par1, at1, u1 = (s, par, at, u - 1) if u else (s - 1, 1 - par, at - 1, 3)
                    if has(at, 0):
                        if has(at1, 0):
                            after(pe, "exp_out", 16, q1, 4 * u1 + 3)
                        scores_for_max(s, par, u)
                    if has(at, 1):
                        if u < 2:
                            if has(at1, 0):
                                after(pe, "mxT_out", 4, q1, u1)
                            xn_transpose(s + 1, u, at + 1)
                        project(s + 1, 1 - par, u, at + 1)
                        if u == 0:
                            if at == 0:
                                after(pe, "V_out", 4, s, 3)
                            if has(at, -2):
                                after(pe, "rk_out", 1, s - 2, 0)
                        q2, u2 = (s, u - 2) if u >= 2 else (s - 1, u + 2)
                        if has(at if u >= 2 else at - 1, 0):
                            after(pe, "x2_out", 4, q2, u2)
                        elif u == 1:
                            after(pe, "V_out", 4, s + 1, 0)
                        values(s + 1, 1 - par, u)
                    if has(at, -1) and u == 3:
                        if has(at, 1):
                            after(pe, "V_out", 4, s + 1, u)
                        q2, u2 = (s, 1)
                        if has(at, 0):
                            after(pe, "x2_out", 4, s, 1)
                        else:
                            after(pe, "x2_out", 4, s - 1, 3)
                        logits(s - 1)
                    if has(at, 0):
                        if has(at, 1) and u < 2:
                            after(pe, "xnT_out", 2, s + 1, u)
                        if has(at, -1) and u >= 2:
                            after(pe, "xn2T_out", 2, s - 1, u - 2)
                        max_transpose(s, u)
                    if has(at1, 0):
                        after(pe, "exp_out", 16, q1, 4 * u1 + 3)
                        q2, u2 = (q1, u1 - 1) if u1 else (q1 - 1, 3)
                        if has(at1 if u1 else at1 - 1, 0):
                            after(pe, "aT_out", 4, q2, u2)
                        attend(q1, par1, u1)
                    if has(at, 0):
                        scores(s, par, u)
                    if has(at1, 0):
                        if has(at, 1):
                            after(pe, "V_out", 4, s + 1, u)
                        if has(at, -1) and u == 3:
                            after(pe, "lg_out", 1, s - 1, 0)
                        if u == 0 and has(at, -2):
                            after(pe, "rk_out", 1, s - 2, 0)
                        if not has(at, 1):
                            q2, u2 = (q1, u1 - 1) if u1 else (q1 - 1, 3)
                            after(pe, "x2_out", 4, q2, u2)
                        project_out(q1, u1)
                    if has(at, -1) and u in (1, 2):
                        if has(at, 0):
                            after(pe, "mxT_out", 4, s, u)
                        elif u == 2:
                            after(pe, "xn2T_out", 2, s - 1, 0)
                        xn2_transpose(s - 1, u - 1)
                    if has(at, -1) and u == 3:
                        if has(at1, 0):
                            after(pe, "x2_out", 4, q1, u1)
                        after(pe, "lg_out", 1, s - 1, 0)
                        ranks(s - 1, 1 - par, at - 1)

            slots(pe, step)

            def page_transpose(n, r, first):
                after(pe, "pn_out", 1, n, 0)
                if not first:
                    after(pe, "pT_out", 1, n - 2, 0)
                bank = b4 if r % 2 == 0 else b5
                for c in range(2):
                    ins = pe.transpose(bank[:, c * P:(c + 1) * P], pn[:, r, c * P:(c + 1) * P], ident)
                ins.then_inc(S["pT_done"], 1)

            def page_first(n, r, first):
                after(pe, "pT_out", 1, n, 0)
                if not first:
                    after(pe, "h_out", 1, n - 2, 0)
                bank = b6 if r % 2 == 0 else b7
                for i in range(2):
                    ins = pe.matmul(bank[0:HID, 0:P], w1s[:, r, i * HID:(i + 1) * HID], pnT[:, r % 2, i * P:(i + 1) * P],
                                    start=(i == 0), stop=(i == 1))
                ins.then_inc(S["h_done"], 1)

            def page_second(n, r, first):
                after(pe, "h_out", 1, n, 0)
                if not first:
                    after(pe, "po_out", 1, n - 2, 0)
                pe.matmul(sc[r % 2][:, 0:D], hT[:, r % 2, :], w2s[:, r, :], start=True, stop=True).then_inc(S["y_done"], 1)

            after(pe, "rk_out", 1, NQ - 1, 0)
            for n in range(2 * PG):
                page_transpose(n, n % PG, n < 2)
                if n >= 1:
                    page_first(n - 1, (n - 1) % PG, n - 1 < 2)
                if n >= 2:
                    page_second(n - 2, (n - 2) % PG, n - 2 < 2)
            with pe.Fori(2, PAGES // PG) as i:
                for r in range(PG):
                    page_transpose(i * PG + r, r, False)
                    page_first(i * PG + (r - 1), (r - 1) % PG, False)
                    page_second(i * PG + (r - 2), (r - 2) % PG, False)
            page_first(PAGES - 1, PG - 1, False)
            page_second(PAGES - 2, PG - 2, False)
            page_second(PAGES - 1, PG - 1, False)


def kernel(**inputs):
    import concourse.bacc as bacc
    from concourse.bass_utils import run_bass_kernel_spmd

    a = {k: np.asarray(v) for k, v in inputs.items()}
    x, c = a["x"], a["ctx_1024"]
    nb, t, d = x.shape

    def columns(w):
        return w.T.reshape(d // P, P, -1).transpose(1, 0, 2)

    def per_feature(v):
        return v.reshape(d // P, P).T

    def on_all(v):
        return np.broadcast_to(v, (P,) + v.shape)

    w1, w2 = a["L0_ffn_weights1"], a["L0_ffn_weights2"]
    e, _, hid = w1.shape
    b1 = np.concatenate([a["L0_ffn_bias1"], np.zeros((e, P - hid), np.float32)], 1)
    arrays = {
        "x_in": x,
        "ctxT": c.reshape(nb // QB, QB, t, d // P, P).transpose(0, 4, 3, 1, 2).reshape(nb // QB, P, d // P, QB * t),
        "wq": columns(a["L0_xattn_Wq"]), "wk": columns(a["L0_xattn_Wk"]),
        "wv": columns(a["L0_xattn_Wv"]), "wo": columns(a["L0_xattn_Wo"]),
        "bq": per_feature(a["L0_xattn_bq"]), "bk": per_feature(a["L0_xattn_bk"]),
        "bv": on_all(a["L0_xattn_bv"]), "bo": on_all(a["L0_xattn_bo"]),
        "wr": columns(a["L0_ffn_router_w"]), "rb": on_all(a["L0_ffn_router_b"]),
        "w1": np.concatenate([w1.reshape(e, d // P, P, hid).transpose(0, 2, 1, 3).reshape(e, P, -1), b1[:, :, None]], 2),
        "w2": np.concatenate([w2, a["L0_ffn_bias2"][:, None, :]], 1),
        "consts": constants(),
    }
    arrays = {k: np.ascontiguousarray(v) for k, v in arrays.items()}
    nc = bacc.Bacc("TRN2", target_bir_lowering=False, num_devices=1)
    args = [nc.dram_tensor(k, v.shape, mybir.dt.from_np(v.dtype), kind="ExternalInput").ap() for k, v in arrays.items()]
    args.append(nc.dram_tensor("out", x.shape, F32, kind="ExternalOutput").ap())
    build(nc, *args)
    r = run_bass_kernel_spmd(nc, [arrays], core_ids=[0])
    return r.results[0]["out"]
```

```python
from contextlib import ExitStack

import numpy as np

import concourse.bass as bass
from concourse import mybir

F32 = mybir.dt.float32
BF16 = mybir.dt.bfloat16
I32 = mybir.dt.int32
U32 = mybir.dt.uint32
ALU = mybir.AluOpType
ACT = mybir.ActivationFunctionType
AX = mybir.AxisListType

P = 128
HD = 16
QB = 4
ROW = 260
COL_TOKEN, COL_EXPERT, COL_MEAN, COL_RSTD = 256, 257, 258, 259
NOWHERE = 1 << 30
EPS = 1e-5
PG = 16
PN = 8
GP = 4
LAG = 4
ROUND = 1.5 * 2.0 ** 23

C_IDENT, C_TRI, C_ONES, C_MASK, C_IOTA, C_TOKEN = 0, 128, 256, 320, 328, 360
C_ALL = 364


def constants():
    c = np.zeros((P, C_ALL), np.float32)
    p = np.arange(P)
    c[:, C_IDENT:C_IDENT + P] = np.eye(P)
    c[:, C_TRI:C_TRI + P] = p[:, None] < p[None, :]
    for m in range(2):
        c[:, C_ONES + 32 * m + 16 * m:C_ONES + 32 * m + 16 * m + 16] = 1.0
    c[:, C_MASK:C_MASK + 8] = p[:, None] // HD == np.arange(8)
    c[:, C_IOTA:C_IOTA + 32] = np.arange(32)
    c[:, C_TOKEN:C_TOKEN + QB] = p[:, None] + P * np.arange(QB)
    return c


def build(nc, x, ctxT, wq, wk, wv, wo, bq, bk, bv, bo, wr, rb, w1, w2, consts, out):
    NB = x.shape[0]
    D = x.shape[2]
    NQ = NB // QB
    E = wr.shape[2]
    HID = w2.shape[0] - 1
    TOKENS = NB * P
    PAGES = -(-(TOKENS // P + E) // PG) * PG
    x_q = x.rearrange("(q b) t d -> q t b d", b=QB)
    out_rows = out.rearrange("b t d -> (b t) d")
    pages = nc.dram_tensor("pages", (PAGES * P, ROW), F32).ap()
    page_view = pages.rearrange("(n p) c -> p n c", p=P)

    ctx = ExitStack()
    with ctx:
        def sb(name, shape, dt=F32):
            return ctx.enter_context(nc.sbuf_tensor(name, [P] + shape, dt))

        def ps(name):
            return ctx.enter_context(nc.psum_tensor(name, [P, 512], F32))

        def sem(name):
            return ctx.enter_context(nc.semaphore(name))

        cst = sb("cst", [C_ALL])
        wq_s, wk_s, wv_s, wo_s = (sb(n, [2, D]) for n in ("wq_s", "wk_s", "wv_s", "wo_s"))
        wr_s = sb("wr_s", [2, P])
        bq_s, bk_s = sb("bq_s", [2]), sb("bk_s", [2])
        bq4 = sb("bq4", [2])
        bkm = sb("bkm", [2, 8])
        bv_s, bo_s = sb("bv_s", [D]), sb("bo_s", [D])
        rb_s = sb("rb_s", [E])
        ident_b, tri_b, ones_b = sb("ident_b", [P], BF16), sb("tri_b", [P], BF16), sb("ones_b", [P], BF16)
        sel_b = sb("sel_b", [16, P], BF16)
        half = sb("half", [QB])
        xs = sb("xs", [2, QB, D])
        xb = sb("xb", [2, QB, D])
        xn = sb("xn", [QB, D])
        xnT = sb("xnT", [2, QB * P])
        cT = sb("cT", [2, 2, QB * P])
        qT = sb("qT", [2, 2, QB * P])
        kM = sb("kM", [2, 2, 8, QB * P])
        qTh = qT[:, :, :, :].bitcast(BF16).rearrange("p a c (t w) -> p a c t w", w=2)[:, :, :, :, 1]
        kMh = kM[:, :, :, :, :].bitcast(BF16).rearrange("p a c h (t w) -> p a c h t w", w=2)[:, :, :, :, :, 1]
        vs = sb("vs", [2, QB, 8, 4, 16])
        mx = sb("mx", [2, P], BF16)
        mxT = sb("mxT", [2, P], BF16)
        pt = sb("pt", [2, 4, 512])
        rz = sb("rz", [2 * P])
        aT = sb("aT", [2, 2, P])
        row = sb("row", [2, QB, ROW])
        st1, ag1, rs1 = sb("st1", [QB, 6]), sb("ag1", [QB, 2]), sb("rs1", [QB])
        st2 = sb("st2", [QB, 6])
        xn2 = sb("xn2", [QB, D])
        xn2T = sb("xn2T", [2, QB * P])
        lg = sb("lg", [QB, E])
        top, topi, idxf = sb("top", [QB, 8]), sb("topi", [QB, 8], U32), sb("idxf", [QB])
        hot = sb("hot", [2, QB, E], BF16)
        seen = sb("seen", [E], BF16)
        rk = sb("rk", [QB + 1, E])
        B = sb("B", [E])
        Doff = sb("Doff", [E])
        T0 = sb("T0", [1])
        fresh, run, noff, dd = sb("fresh", [E]), sb("run", [E]), sb("noff", [E]), sb("dd", [E])
        zer = sb("zer", [E])
        t1, t2 = sb("t1", [QB, E]), sb("t2", [QB, E])
        grew, shift = sb("grew", [E]), sb("shift", [E])
        slot = sb("slot", [QB])
        slot_i = sb("slot_i", [2, QB], U32)
        tok = sb("tok", [QB])
        tsum = sb("tsum", [E])
        empty = sb("empty", [ROW])
        table = ctx.enter_context(nc.sbuf_tensor("table", [1, PAGES], I32))
        w1s = sb("w1s", [E, 2 * HID + 1])
        w1p = row[:, :, :, :].rearrange("p a u c -> p (a u c)")[:, 0:PN * (2 * HID + 1)].rearrange("p (n c) -> p n c", n=PN)
        w2p = xs[0:HID + 1].rearrange("p a u d -> p (a u) d")
        w2s = kM[0:HID + 1, 0].rearrange("p c h (g d) -> p (c h g) d", d=D)
        pr = kM[:, 1].rearrange("p c h t -> p (c h t)")[:, 0:PG * ROW].rearrange("p (n c) -> p n c", c=ROW)
        pn = cT[:, :, :, :].rearrange("p a c t -> p (a c t)")[:, 0:PN * D].rearrange("p (n c) -> p n c", c=D)
        pnT = sb("pnT", [2, 2 * P])
        hT = ctx.enter_context(nc.sbuf_tensor("hT", [HID + 1, 2, P], F32))

        sc = [ps(f"sc{j}") for j in range(4)]
        b4, b5, b6, b7 = ps("b4"), ps("b5"), ps("b6"), ps("b7")
        b5h = b5[:, :].bitcast(BF16)

        names = """ld_w ld_w2 fill ld_x0 ld_x1 ld_c0 ld_c1 table_in page_in0 page_in1 page_in2 page_in3 page_in4 page_in5 page_in6 page_in7
          scattered wrote0 wrote1 wrote2 wrote3 wrote4 wrote5 wrote6 wrote7 ld_w1 ld_experts
          cst_ready pool_init dve_init
          S_done xnT_done proj_done V_done mxT_done PV_done T_done O_done xn2T_done lg_done rk_done
          xnT_out proj_out exp_out xn2T_out
          max_out V_out lg_out mxT_out inv_out aT_out x2_out stat2_out agg2_out xn2_out
          stat1_out agg1_out xn_out top_out topi_out idx_out hot_out rk_out tsum_out seen_out
          need_out need_frac need_round pages_run pages_first fresh_start fresh_shift
          in_fresh old_slot fresh_step slot_each slot_own slot_sum page_total grew_out B_out shift_out D_out slot_out tok_next
          var2_out rstd2_out var1_out rstd1_out xb_out tok_out
          pn_out pT_done h_done y_done pT_out h_out po_out""".split()
        S = {n: sem(n) for n in names}

        def after(eng, name, per, q, k):
            eng.wait_ge(S[name], q * per + (k + 1))

        def apart(eng, *waits):
            waits = [(S[name], value if isinstance(value, int) else eng.to_reg(value)) for name, value in waits]
            eng.wait_ge(*settled[eng.engine])
            for semaphore, value in waits:
                eng.wait_ge(semaphore, value)

        def arrived(eng, name, q, par):
            eng.wait_ge(S[f"{name}{par}"], (q - par) * 8 + 16)

        ET = mybir.EngineType
        settled = {ET.DVE: (S["dve_init"], 6), ET.Pool: (S["pool_init"], 7), ET.SP: (S["pool_init"], 6)}

        block = ctx.enter_context(nc.Block())
        LO, HI = 2, NQ - 2

        def slots(eng, step):
            for s in range(LO):
                step(s, s % 2, s)
            with eng.Fori(0, (HI - LO) // 2) as i:
                for k in range(2):
                    step(i * 2 + (LO + k), k, LO)
            for s in range(HI, NQ + 2):
                step(s, s % 2, s)

        def has(at, lead):
            return 0 <= at + lead < NQ

        @block.sync
        def _(sp):
            for dst, src in ((cst[:, :], consts), (wk_s[:, :, :], wk), (wv_s[:, :, :], wv),
                             (wq_s[:, :, :], wq), (bq_s[:, :], bq), (bk_s[:, :], bk), (bv_s[:, :], bv)):
                sp.dma_start(dst, src).then_inc(S["ld_w"], 16)

            def load(q, par, at):
                if at >= 2:
                    apart(sp, ("xn_out", q * 4 - 4), ("xb_out", q - 1))
                sp.dma_start(xs[:, par], x_q[bass.ds(q, 1)].rearrange("a t b d -> t (a b) d")).then_inc(S[f"ld_x{par}"], 16)
                if at >= 2:
                    apart(sp, ("proj_done", q * 4 - 6), ("V_done", q * 4 - 4))
                sp.dma_start(cT[:, par], ctxT[bass.ds(q, 1)].rearrange("a p c t -> p (a c) t")).then_inc(S[f"ld_c{par}"], 16)

            load(0, 0, 0)
            for dst, src in ((wo_s[:, :, :], wo), (bo_s[:, :], bo), (rb_s[:, :], rb)):
                sp.dma_start(dst, src).then_inc(S["ld_w2"], 16)
            sp.wait_ge(S["pool_init"], 6)
            sp.dma_start(wr_s[:, :, 0:E], wr).then_inc(S["ld_w2"], 16)
            load(1, 1, 1)
            sp.dma_start(w1s[:, :, :], w1).then_inc(S["ld_experts"], 16)
            with sp.Fori(0, (NQ - 2) // 2) as i:
                for k in range(2):
                    load(i * 2 + (2 + k), k, 2)

            sp.wait_ge(S["T_done"], 16 * (NQ - 1))
            sp.dma_start(w2s, w2).then_inc(S["ld_experts"], 16)
            sp.wait_ge(S["scattered"], 64 * NQ)
            with nc.allow_non_contiguous_dma(reason="one word of each page"):
                sp.dma_start(table[0:1, :], pages.rearrange("(n p) c -> n p c", p=P)[:, 0, COL_EXPERT:COL_EXPERT + 1]
                             .rearrange("n c -> c n").bitcast(I32)).then_inc(S["table_in"], 16)

            def load_pages(n, r, first):
                if not first:
                    sp.wait_ge(S[f"wrote{r // GP}"], (n - r) * (16 * GP // PG))
                sp.dma_start(pr[:, r:r + GP, :], page_view[:, bass.ds(n, GP), :]).then_inc(S[f"page_in{r // GP}"], 16)

            for n in range(0, PG, GP):
                load_pages(n, n, True)
            with sp.Fori(1, PAGES // PG) as i:
                for r in range(0, PG, GP):
                    load_pages(i * PG + r, r, False)
            for g in range(PG // GP):
                sp.wait_ge(S[f"wrote{g}"], 16 * GP * (PAGES // PG))

        @block.gpsimd
        def _(pool):
            pool.memset(empty[:, :], 0.0).then_inc(S["pool_init"], 1)
            pool.memset(vs[:, :, :, :, :, :], 0.0).then_inc(S["pool_init"], 1)
            pool.memset(mx[:, :, :], 0.0).then_inc(S["pool_init"], 1)
            pool.memset(seen[:, :], 0.0).then_inc(S["pool_init"], 1)
            pool.memset(half[:, :], -0.5).then_inc(S["pool_init"], 1)
            pool.memset(wr_s[:, :, :], 0.0).then_inc(S["pool_init"], 1)
            pool.wait_ge(S["pool_init"], 6)
            pool.memset(empty[:, COL_TOKEN:COL_TOKEN + 1].bitcast(I32), NOWHERE).then_inc(S["pool_init"], 1)
            pool.wait_ge(S["pool_init"], 7)
            NF = 8
            for f in range(NF):
                n = PAGES // NF
                pool.dma_start(page_view[:, n * f:n * (f + 1), :],
                               empty[:, :].unsqueeze(1).to_broadcast([P, n, ROW])).then_inc(S["fill"], 16)

            last_slot, last_token = pool.to_reg(PAGES * P - 1), pool.to_reg(TOKENS - 1)

            def rstd1(q):
                apart(pool, ("agg1_out", q * 4 + 4))
                pool.tensor_scalar(rs1[:, :], ag1[:, :, 1], EPS, None, ALU.add).then_inc(S["var1_out"], 1)
                after(pool, "var1_out", 1, q, 0)
                pool.tensor_tensor(rs1[:, :], rs1[:, :], half[:, :], ALU.pow).then_inc(S["rstd1_out"], 1)

            def rstd2(q, par):
                apart(pool, ("agg2_out", q * 4 + 4))
                v = row[:, par, :, COL_RSTD]
                pool.tensor_scalar(v, v, EPS, None, ALU.add).then_inc(S["var2_out"], 1)
                after(pool, "var2_out", 1, q, 0)
                pool.tensor_tensor(v, v, half[:, :], ALU.pow).then_inc(S["rstd2_out"], 1)

            def add_bo(q, par, at):
                if at == 0:
                    pool.wait_ge(S["ld_w2"], 64)
                arrived(pool, "ld_x", q, par)
                if at >= 2:
                    after(pool, "x2_out", 4, q - 2, 3)
                pool.tensor_tensor(xb[:, par], xs[:, par], bo_s[:, :].unsqueeze(1).to_broadcast([P, QB, D]),
                                   ALU.add).then_inc(S["xb_out"], 1)

            def scatter(q, par, at):
                if at == 0:
                    pool.wait_ge(S["fill"], 16 * NF)
                apart(pool, ("slot_out", q + 1))
                for u in range(QB):
                    pool.indirect_dma_start(
                        pages, bass.IndirectOffsetOnAxis(slot_i[:, par, u:u + 1], 0), row[:, par, u, :], None,
                        bounds_check=last_slot, oob_is_err=False).then_inc(S["scattered"], 16)

            rstd1(0)
            add_bo(0, 0, 0)
            rstd1(1)

            def step(s, par, at):
                if has(at, 2):
                    rstd1(s + 2)
                if has(at, -2):
                    scatter(s - 2, par, at - 2)
                if has(at, -1):
                    rstd2(s - 1, 1 - par)
                if has(at, 1):
                    add_bo(s + 1, 1 - par, at + 1)

            slots(pool, step)

            def write_page(n, r):
                apart(pool, ("po_out", n + 1))
                pool.indirect_dma_start(
                    out_rows, bass.IndirectOffsetOnAxis(pr[:, r, COL_TOKEN:COL_TOKEN + 1].bitcast(U32), 0),
                    pr[:, r, 0:D], None, bounds_check=last_token, oob_is_err=False).then_inc(S[f"wrote{r // GP}"], 16)

            with pool.Fori(0, PAGES // PG) as i:
                for r in range(PG):
                    write_page(i * PG + r, r)

        @block.scalar
        def _(act):
            act.wait_ge(S["cst_ready"], 6)

            def xnT_copy(q, h, at):
                after(act, "xnT_done", 2, q, h)
                if at >= 1:
                    after(act, "proj_done", 4, q - 1, 3)
                src = b5[:, :].rearrange("p (u c t) -> p c u t", u=2, c=2)
                dst = xnT[:, :, 2 * P * h:2 * P * (h + 1)].rearrange("p c (u t) -> p c u t", u=2)
                for c in range(2):
                    ins = act.activation(dst[:, c], src[:, c], ACT.Copy)
                ins.then_inc(S["xnT_out"], 1)

            def proj_copy(q, par, k, at):
                after(act, "proj_done", 4, q, k)
                if at >= 2:
                    after(act, "T_done", 16, q - 2, 15)
                if k < 2:
                    for h in range(8):
                        ins = act.activation(kM[:, par, k, h], b4[:, :], ACT.Identity, bias=bkm[:, k, h:h + 1],
                                             scale=cst[:, C_MASK + h:C_MASK + h + 1])
                    ins.then_inc(S["proj_out"], 1)
                else:
                    c = k - 2
                    act.activation(qT[:, par, c], b4[:, :], ACT.Identity, bias=bq4[:, c:c + 1], scale=0.25).then_inc(S["proj_out"], 1)

            def exps(q, u, at):
                for j in range(4):
                    after(act, "T_done", 16, q, 4 * u + j)
                    if j == 0 and (at >= 1 or u >= 2):
                        qq, uu = (q, u - 2) if u >= 2 else (q - 1, u + 2)
                        after(act, "PV_done", 4, qq, uu)
                    act.activation(pt[:, u % 2, j], sc[j][:, :], ACT.Exp).then_inc(S["exp_out"], 1)

            def xn2T_copy(q, h, at):
                after(act, "xn2T_done", 2, q, h)
                if at >= 1:
                    after(act, "lg_done", 1, q - 1, 0)
                src = b5[:, :].rearrange("p (u c t) -> p c u t", u=2, c=2)
                dst = xn2T[:, :, 2 * P * h:2 * P * (h + 1)].rearrange("p c (u t) -> p c u t", u=2)
                for c in range(2):
                    ins = act.activation(dst[:, c], src[:, c], ACT.Copy)
                ins.then_inc(S["xn2T_out"], 1)

            xnT_copy(0, 0, 0)
            xnT_copy(0, 1, 0)
            for k in range(4):
                proj_copy(0, 0, k, 0)

            def step(s, par, at):
                for u in range(QB):
                    if has(at, 1):
                        if u < 2:
                            xnT_copy(s + 1, u, at + 1)
                        proj_copy(s + 1, 1 - par, u, at + 1)
                    if has(at, -1) and u == 1:
                        xn2T_copy(s - 1, 0, at - 1)
                    if has(at, 0):
                        exps(s, u, at)
                    if has(at, -1) and u == 1:
                        xn2T_copy(s - 1, 1, at - 1)

            slots(act, step)

            def pnT_copy(n, r):
                after(act, "pT_done", 1, n, 0)
                act.activation(pnT[:, r % 2, :], b4[:, 0:256] if r % 2 == 0 else b5[:, 0:256], ACT.Copy).then_inc(S["pT_out"], 1)

            def h_copy(n, r, first):
                after(act, "h_done", 1, n, 0)
                if not first:
                    after(act, "y_done", 1, n - 2, 0)
                act.activation(hT[0:HID, r % 2, :], b6[0:HID, 0:P] if r % 2 == 0 else b7[0:HID, 0:P], ACT.Relu,
                               bias=w1p[0:HID, r % PN, 2 * HID:2 * HID + 1]).then_inc(S["h_out"], 1)

            for n in range(PG):
                pnT_copy(n, n)
                if n >= 1:
                    h_copy(n - 1, n - 1, n - 1 < 2)
            with act.Fori(1, PAGES // PG) as i:
                for r in range(PG):
                    pnT_copy(i * PG + r, r)
                    h_copy(i * PG + (r - 1), (r - 1) % PG, False)
            h_copy(PAGES - 1, PG - 1, False)

        @block.vector
        def _(dve):
            dve.wait_ge(S["ld_w"], 16 * 7)
            dve.memset(ones_b[:, :], 1.0).then_inc(S["cst_ready"], 1)
            dve.tensor_copy(ident_b[:, :], cst[:, C_IDENT:C_IDENT + P]).then_inc(S["cst_ready"], 1)
            dve.tensor_copy(tri_b[:, :], cst[:, C_TRI:C_TRI + P]).then_inc(S["cst_ready"], 1)
            dve.tensor_scalar(sel_b[:, :, :], cst[:, C_IDENT:C_IDENT + 16].unsqueeze(2).to_broadcast([P, 16, P]), -1.0, None,
                              ALU.mult).then_inc(S["cst_ready"], 1)
            for c in range(2):
                ins = dve.tensor_scalar(bkm[:, c, :], cst[:, C_MASK:C_MASK + 8], bk_s[:, c:c + 1], None, ALU.mult)
            ins.then_inc(S["cst_ready"], 1)
            dve.tensor_scalar(bq4[:, :], bq_s[:, :], 0.25, None, ALU.mult).then_inc(S["cst_ready"], 1)
            dve.memset(B[:, :], 0.0).then_inc(S["dve_init"], 1)
            dve.memset(Doff[:, :], 0.0).then_inc(S["dve_init"], 1)
            dve.memset(T0[:, :], 0.0).then_inc(S["dve_init"], 1)
            dve.memset(zer[:, :], 0.0).then_inc(S["dve_init"], 1)
            dve.memset(hT[:, :, :], 1.0).then_inc(S["dve_init"], 1)
            dve.tensor_copy(tok[:, :], cst[:, C_TOKEN:C_TOKEN + QB]).then_inc(S["dve_init"], 1)
            dve.wait_ge(S["dve_init"], 6)

            def stats1(q, par):
                arrived(dve, "ld_x", q, par)
                for u in range(QB):
                    dve.bn_stats(st1[:, u, :], xs[:, par, u, :]).then_inc(S["stat1_out"], 1)
                for u in range(QB):
                    apart(dve, ("stat1_out", q * 4 + (u + 1)))
                    dve.bn_aggr(ag1[:, u, :], st1[:, u, :]).then_inc(S["agg1_out"], 1)

            def norm1(q, par, at):
                after(dve, "rstd1_out", 1, q, 0)
                if at >= 1:
                    after(dve, "xnT_done", 2, q - 1, 1)
                for u in range(QB):
                    dve.tensor_scalar(xn[:, u, :], xs[:, par, u, :], ag1[:, u, 0:1], rs1[:, u:u + 1],
                                      ALU.subtract, ALU.mult).then_inc(S["xn_out"], 1)

            def maxima(q, u, at):
                if at >= 1 or u >= 2:
                    qq, uu = (q, u - 2) if u >= 2 else (q - 1, u + 2)
                    after(dve, "mxT_done", 4, qq, uu)
                after(dve, "S_done", 4, q, u)
                for j in range(4):
                    ins = dve.tensor_reduce(mx[:, u % 2, 4 * j:4 * j + 4], sc[j][:, :].rearrange("p (h k) -> p h k", h=4), AX.X, ALU.max)
                ins.then_inc(S["max_out"], 1)

            def v_copy(q, par, u, at):
                after(dve, "V_done", 4, q, u)
                if at >= 2:
                    after(dve, "PV_done", 4, q - 2, u)
                for m in range(2):
                    ins = dve.tensor_tensor(
                        vs[:, par, u, :, 3 * m, :], b6[:, 0:D].rearrange("p (g m d) -> p g m d", g=8, m=2)[:, :, m, :],
                        bv_s[:, :].rearrange("p (g m d) -> p g m d", g=8, m=2)[:, :, m, :], ALU.add)
                ins.then_inc(S["V_out"], 1)

            def mxT_copy(q, u, at):
                after(dve, "mxT_done", 4, q, u)
                dve.tensor_copy(mxT[:, u % 2, :], b5h[:, 0:P]).then_inc(S["mxT_out"], 1)

            def attend_copy(q, u, at):
                after(dve, "PV_done", 4, q, u)
                dve.reciprocal(rz[:, :], b7[:, 2 * P:4 * P]).then_inc(S["inv_out"], 1)
                after(dve, "inv_out", 4, q, u)
                if at >= 1 or u >= 2:
                    qq, uu = (q, u - 2) if u >= 2 else (q - 1, u + 2)
                    after(dve, "O_done", 4, qq, uu)
                dve.tensor_tensor(aT[:, u % 2].rearrange("p c t -> p (c t)"), b7[:, 0:2 * P], rz[:, :], ALU.mult).then_inc(S["aT_out"], 1)

            def residual(q, par, u, at):
                after(dve, "O_done", 4, q, u)
                after(dve, "xb_out", 1, q, 0)
                if at >= 2 and u == 0:
                    dve.wait_ge(S["scattered"], (q - 1) * 64)
                dve.tensor_tensor(row[:, par, u, 0:D], b6[:, D:2 * D], xb[:, par, u, :], ALU.add).then_inc(S["x2_out"], 1)
                after(dve, "x2_out", 4, q, u)
                dve.bn_stats(st2[:, u, :], row[:, par, u, 0:D]).then_inc(S["stat2_out"], 1)
                apart(dve, ("stat2_out", q * 4 + (u + 1)))
                dve.bn_aggr(row[:, par, u, COL_MEAN:COL_MEAN + 2], st2[:, u, :]).then_inc(S["agg2_out"], 1)

            def norm2(q, par, at):
                after(dve, "rstd2_out", 1, q, 0)
                if at >= 1:
                    after(dve, "xn2T_done", 2, q - 1, 1)
                for u in range(QB):
                    dve.tensor_scalar(xn2[:, u, :], row[:, par, u, 0:D], row[:, par, u, COL_MEAN:COL_MEAN + 1],
                                      row[:, par, u, COL_RSTD:COL_RSTD + 1], ALU.subtract, ALU.mult).then_inc(S["xn2_out"], 1)

            def logits(q):
                after(dve, "lg_done", 1, q, 0)
                dve.tensor_tensor(lg[:, :, :], b6[:, :].rearrange("p (u k) -> p u k", u=QB)[:, :, 0:E],
                                  rb_s[:, :].unsqueeze(1).to_broadcast([P, QB, E]), ALU.add).then_inc(S["lg_out"], 1)

            def choose(q):
                apart(dve, ("lg_out", q + 1))
                for u in range(QB):
                    dve.max(top[:, u, :], lg[:, u, :]).then_inc(S["top_out"], 1)
                for u in range(QB):
                    apart(dve, ("top_out", q * 4 + (u + 1)))
                    dve.max_index(topi[:, u, :], top[:, u, :], lg[:, u, :]).then_inc(S["topi_out"], 1)

            def one_hot(q, par, at):
                after(dve, "topi_out", 4, q, 3)
                dve.tensor_copy(idxf[:, :], topi[:, :, 0]).then_inc(S["idx_out"], 1)
                dve.tensor_copy(row[:, par, :, COL_EXPERT].bitcast(U32), topi[:, :, 0])
                dve.tensor_copy(row[:, par, :, COL_TOKEN].bitcast(I32), tok[:, :]).then_inc(S["tok_out"], 1)
                after(dve, "idx_out", 1, q, 0)
                dve.tensor_tensor(hot[:, par], cst[:, C_IOTA:C_IOTA + E].unsqueeze(1).to_broadcast([P, QB, E]),
                                  idxf[:, :].unsqueeze(2).to_broadcast([P, QB, E]), ALU.is_equal).then_inc(S["hot_out"], 1)
                after(dve, "tok_out", 1, q, 0)
                dve.tensor_scalar(tok[:, :], tok[:, :], float(QB * P), None, ALU.add).then_inc(S["tok_next"], 1)

            def rank_copy(q, par):
                after(dve, "rk_done", 1, q, 0)
                dve.tensor_copy(rk[:, :, :].rearrange("p u e -> p (u e)"), b6[:, 0:(QB + 1) * E]).then_inc(S["rk_out"], 1)
                after(dve, "hot_out", 1, q, 0)
                dve.tensor_reduce(tsum[:, :], hot[:, par].rearrange("p u e -> p e u"), AX.X, ALU.add).then_inc(S["tsum_out"], 1)
                after(dve, "tok_next", 1, q, 0)
                after(dve, "tsum_out", 1, q, 0)
                dve.tensor_tensor(seen[:, :], seen[:, :], tsum[:, :], ALU.add).then_inc(S["seen_out"], 1)
                after(dve, "seen_out", 1, q, 0)

            def own(name, q, ins):
                ins.then_inc(S[name], 1)
                after(dve, name, 1, q, 0)

            def each(t):
                return t[:, :].unsqueeze(1).to_broadcast([P, QB, E])

            def fresh_pages(q):
                after(dve, "rk_out", 1, q, 0)
                rank, count = rk[:, 0:QB, :], rk[:, QB, :]
                own("need_out", q, dve.tensor_tensor(fresh[:, :], count, B[:, :], ALU.subtract))
                dve.tensor_tensor(t1[:, :, :], rank, each(B), ALU.is_ge).then_inc(S["in_fresh"], 1)
                own("need_frac", q, dve.tensor_scalar(fresh[:, :], fresh[:, :], 1.0 / P, (P - 1.0) / (2 * P), ALU.mult, ALU.add))
                dve.tensor_tensor(t2[:, :, :], rank, each(Doff), ALU.add).then_inc(S["old_slot"], 1)
                own("need_round", q, dve.tensor_scalar(fresh[:, :], fresh[:, :], ROUND, ROUND, ALU.add, ALU.subtract))
                own("pages_run", q, dve.tensor_tensor_scan(run[:, :], fresh[:, :], zer[:, :], T0[:, 0:1], ALU.add, ALU.add))
                dve.tensor_copy(T0[:, 0:1], run[:, E - 1:E]).then_inc(S["page_total"], 1)
                own("pages_first", q, dve.tensor_tensor(noff[:, :], run[:, :], fresh[:, :], ALU.subtract))
                own("fresh_start", q, dve.scalar_tensor_tensor(noff[:, :], noff[:, :], float(P), B[:, :], ALU.mult, ALU.subtract))
                own("fresh_shift", q, dve.tensor_tensor(dd[:, :], noff[:, :], Doff[:, :], ALU.subtract))

            def place(q, par):
                after(dve, "in_fresh", 1, q, 0)
                own("fresh_step", q, dve.tensor_tensor(t1[:, :, :], t1[:, :, :], each(dd), ALU.mult))
                after(dve, "old_slot", 1, q, 0)
                own("slot_each", q, dve.tensor_tensor(t1[:, :, :], t1[:, :, :], t2[:, :, :], ALU.add))
                dve.tensor_scalar(grew[:, :], fresh[:, :], 1.0, None, ALU.min).then_inc(S["grew_out"], 1)
                dve.scalar_tensor_tensor(B[:, :], fresh[:, :], float(P), B[:, :], ALU.mult, ALU.add).then_inc(S["B_out"], 1)
                own("slot_own", q, dve.tensor_tensor(t1[:, :, :], t1[:, :, :], hot[:, par], ALU.mult))
                after(dve, "grew_out", 1, q, 0)
                dve.tensor_tensor(shift[:, :], grew[:, :], dd[:, :], ALU.mult).then_inc(S["shift_out"], 1)
                own("slot_sum", q, dve.tensor_reduce(slot[:, :], t1[:, :, :], AX.X, ALU.add))
                dve.tensor_copy(slot_i[:, par, :], slot[:, :]).then_inc(S["slot_out"], 1)
                after(dve, "shift_out", 1, q, 0)
                own("D_out", q, dve.tensor_tensor(Doff[:, :], Doff[:, :], shift[:, :], ALU.add))
                after(dve, "B_out", 1, q, 0)
                after(dve, "page_total", 1, q, 0)

            stats1(0, 0)
            norm1(0, 0, 0)
            dve.wait_ge(S["pool_init"], 3)
            for u in range(QB):
                v_copy(0, 0, u, 0)
            stats1(1, 1)
            norm1(1, 1, 1)

            def step(s, par, at):
                for u in range(QB):
                    if has(at, 0):
                        maxima(s, u, at)
                    if has(at, 1):
                        v_copy(s + 1, 1 - par, u, at + 1)
                    if has(at, 0):
                        mxT_copy(s, u, at)
                    if has(at, 2) and u == 0:
                        stats1(s + 2, par)
                    if has(at, -1) and u == 1:
                        norm2(s - 1, 1 - par, at - 1)
                    if has(at, -1) and u == 3:
                        one_hot(s - 1, 1 - par, at - 1)
                    if has(at, 2) and u == 3:
                        norm1(s + 2, par, at + 2)
                    q1, par1, at1, u1 = (s, par, at, u - 1) if u else (s - 1, 1 - par, at - 1, 3)
                    if has(at1, 0):
                        attend_copy(q1, u1, at1)
                    if has(at, -1) and u == 2:
                        logits(s - 1)
                        choose(s - 1)
                    if has(at, -1) and u == 3:
                        rank_copy(s - 1, 1 - par)
                        fresh_pages(s - 1)
                    if has(at, -2) and u == 0:
                        place(s - 2, par)
                    if has(at1, 0):
                        residual(q1, par1, u1, at1)

            slots(dve, step)

            def page_norm(n, r):
                e = dve.value_load(table[0:1, bass.ds(n, 1)], min_val=0, max_val=E - 1)
                dve.tensor_copy(w1p[:, r % PN, :], w1s[:, bass.ds(e, 1), :].rearrange("p e h -> p (e h)"))
                dve.tensor_copy(w2p[:, r % PN, :], w2s[:, bass.ds(e, 1), :].rearrange("p e d -> p (e d)"))
                if r % GP == 0:
                    dve.wait_ge(S[f"page_in{r // GP}"], (n - r) * (16 // PG) + 16)
                dve.tensor_scalar(pn[:, r % PN, :], pr[:, r, 0:D], pr[:, r, COL_MEAN:COL_MEAN + 1],
                                  pr[:, r, COL_RSTD:COL_RSTD + 1], ALU.subtract, ALU.mult).then_inc(S["pn_out"], 1)

            def page_out(n, r):
                after(dve, "y_done", 1, n, 0)
                dve.scalar_tensor_tensor(pr[:, r, 0:D], sc[r % 4][:, 0:D], 0.0, pr[:, r, 0:D], ALU.max, ALU.add).then_inc(S["po_out"], 1)

            dve.wait_ge(S["table_in"], 16)
            dve.wait_ge(S["ld_experts"], 32)
            for n in range(PG):
                page_norm(n, n)
                if n >= LAG:
                    page_out(n - LAG, n - LAG)
            with dve.Fori(1, PAGES // PG) as i:
                for r in range(PG):
                    page_norm(i * PG + r, r)
                    page_out(i * PG + (r - LAG), (r - LAG) % PG)
            for n in range(PAGES - LAG, PAGES):
                page_out(n, n % PG)

        @block.tensor
        def _(pe):
            ident = cst[:, C_IDENT:C_IDENT + P]
            pe.wait_ge(S["cst_ready"], 6)

            def xn_transpose(q, h, at):
                after(pe, "xn_out", 4, q, 2 * h + 1)
                if h == 1:
                    after(pe, "xnT_out", 2, q, 0)
                for v in range(2):
                    for c in range(2):
                        ins = pe.transpose(b5[:, (2 * v + c) * P:(2 * v + c + 1) * P], xn[:, 2 * h + v, c * P:(c + 1) * P], ident)
                ins.then_inc(S["xnT_done"], 1)

            def project(q, par, k, at):
                c = k % 2
                w, src = (wk_s, cT[:, par]) if k < 2 else (wq_s, xnT)
                if k == 0:
                    arrived(pe, "ld_c", q, par)
                if k == 2:
                    after(pe, "xnT_out", 2, q, 1)
                if k > 0:
                    after(pe, "proj_out", 4, q, k - 1)
                elif at >= 1:
                    after(pe, "proj_out", 4, q - 1, 3)
                for i in range(2):
                    ins = pe.matmul(b4[:, :], w[:, i, c * P:(c + 1) * P], src[:, i, :], start=(i == 0), stop=(i == 1))
                ins.then_inc(S["proj_done"], 1)

            def values(q, par, u):
                if u == 0:
                    arrived(pe, "ld_c", q, par)
                for i in range(2):
                    ins = pe.matmul(b6[:, 0:D], cT[:, par, i, u * P:(u + 1) * P], wv_s[:, i, :], start=(i == 0), stop=(i == 1))
                ins.then_inc(S["V_done"], 1)

            def scores_for_max(q, par, u):
                if u == 0:
                    after(pe, "proj_out", 4, q, 3)
                for j in range(4):
                    ins = pe.matmul(sc[j][:, :], qTh[:, par, j // 2, u * P:(u + 1) * P],
                                    kMh[:, par, j // 2, 4 * (j % 2):4 * (j % 2) + 4, u * P:(u + 1) * P], start=True, stop=True)
                ins.then_inc(S["S_done"], 1)

            def max_transpose(q, u):
                after(pe, "max_out", 4, q, u)
                pe.transpose(b5h[:, 0:P], mx[:, u % 2, :], ident_b[:, :]).then_inc(S["mxT_done"], 1)

            def scores(q, par, u):
                after(pe, "mxT_out", 4, q, u)
                for j in range(4):
                    for h in range(4 * j, 4 * j + 4):
                        pe.matmul(sc[j][:, h % 4 * P:(h % 4 + 1) * P], kM[:, par, h // 8, h % 8, u * P:(u + 1) * P],
                                  qT[:, par, h // 8, u * P:(u + 1) * P], start=True, stop=False)
                        ins = pe.matmul(sc[j][:, h % 4 * P:(h % 4 + 1) * P], sel_b[:, h, :], mxT[:, u % 2, :], start=False, stop=True)
                    ins.then_inc(S["T_done"], 1)

            def attend(q, par, u):
                for part in range(2):
                    for c in range(2):
                        for m in range(2):
                            for j in range(4):
                                h = 8 * c + 2 * j + m
                                w = (vs[:, par, u, 4 * c + j].rearrange("p a d -> p (a d)")[:, 32 * m:32 * m + 32] if part == 0
                                     else cst[:, C_ONES + 32 * m:C_ONES + 32 * m + 32])
                                ins = pe.matmul(b7[32 * j:32 * j + 32, (2 * part + c) * P:(2 * part + c + 1) * P], w,
                                                pt[:, u % 2, h // 4, h % 4 * P:(h % 4 + 1) * P], start=(m == 0), stop=(m == 1))
                ins.then_inc(S["PV_done"], 1)

            def project_out(q, u):
                after(pe, "aT_out", 4, q, u)
                for i in range(2):
                    ins = pe.matmul(b6[:, D:2 * D], aT[:, u % 2, i, :], wo_s[:, i, :], start=(i == 0), stop=(i == 1))
                ins.then_inc(S["O_done"], 1)

            def xn2_transpose(q, h):
                after(pe, "xn2_out", 4, q, 2 * h + 1)
                for v in range(2):
                    for c in range(2):
                        ins = pe.transpose(b5[:, (2 * v + c) * P:(2 * v + c + 1) * P], xn2[:, 2 * h + v, c * P:(c + 1) * P], ident)
                ins.then_inc(S["xn2T_done"], 1)

            def logits(q):
                after(pe, "xn2T_out", 2, q, 1)
                for u in range(QB):
                    for i in range(2):
                        ins = pe.matmul(b6[:, u * P:(u + 1) * P], xn2T[:, i, u * P:(u + 1) * P], wr_s[:, i, :],
                                        start=(i == 0), stop=(i == 1))
                ins.then_inc(S["lg_done"], 1)

            def ranks(q, par, at):
                after(pe, "hot_out", 1, q, 0)
                if at >= 1:
                    after(pe, "seen_out", 1, q - 1, 0)
                pe.matmul(b6[:, 0:QB * E], ones_b[:, :], seen[:, :].unsqueeze(1).to_broadcast([P, QB, E]), start=True, stop=False)
                for v in range(QB - 1):
                    pe.matmul(b6[:, (v + 1) * E:QB * E], ones_b[:, :], hot[:, par, v:v + 1].to_broadcast([P, QB - 1 - v, E]),
                              start=False, stop=False, skip_group_check=True)
                pe.matmul(b6[:, 0:QB * E], tri_b[:, :], hot[:, par], start=False, stop=True)
                pe.matmul(b6[:, QB * E:(QB + 1) * E], ones_b[:, :], seen[:, :], start=True, stop=False)
                for v in range(QB):
                    ins = pe.matmul(b6[:, QB * E:(QB + 1) * E], ones_b[:, :], hot[:, par, v], start=False, stop=(v == QB - 1))
                ins.then_inc(S["rk_done"], 1)

            xn_transpose(0, 0, 0)
            xn_transpose(0, 1, 0)
            for k in range(4):
                project(0, 0, k, 0)
            for u in range(QB):
                if u:
                    after(pe, "V_out", 4, 0, u - 1)
                values(0, 0, u)
            pe.wait_ge(S["ld_w2"], 64)

            def step(s, par, at):
                for u in range(QB):
                    q1, par1, at1, u1 = (s, par, at, u - 1) if u else (s - 1, 1 - par, at - 1, 3)

                    def residual_read():
                        q2, u2 = (q1, u1 - 1) if u1 else (q1 - 1, 3)
                        if has(at1 if u1 else at1 - 1, 0):
                            after(pe, "x2_out", 4, q2, u2)

                    if has(at, 0):
                        if u == 0:
                            after(pe, "V_out", 4, s, 3)
                        if has(at1, 0):
                            after(pe, "exp_out", 16, q1, 4 * u1 + 3)
                        scores_for_max(s, par, u)
                    if has(at, 1):
                        if u < 2:
                            if has(at1, 0):
                                after(pe, "mxT_out", 4, q1, u1)
                            xn_transpose(s + 1, u, at + 1)
                        project(s + 1, 1 - par, u, at + 1)
                        if u > 0:
                            after(pe, "V_out", 4, s + 1, u - 1)
                        elif has(at, -2):
                            after(pe, "rk_out", 1, s - 2, 0)
                        if u == 3 and has(at, -1):
                            after(pe, "lg_out", 1, s - 1, 0)
                        residual_read()
                        values(s + 1, 1 - par, u)
                    if has(at, 0):
                        if has(at, 1) and u < 2:
                            after(pe, "xnT_out", 2, s + 1, u)
                        if has(at, -1) and u == 2:
                            after(pe, "xn2T_out", 2, s - 1, 1)
                        max_transpose(s, u)
                    if has(at1, 0):
                        after(pe, "exp_out", 16, q1, 4 * u1 + 3)
                        q2, u2 = (q1, u1 - 1) if u1 else (q1 - 1, 3)
                        if has(at1 if u1 else at1 - 1, 0):
                            after(pe, "aT_out", 4, q2, u2)
                        attend(q1, par1, u1)
                    if has(at, -1):
                        if u == 1:
                            if has(at, 0):
                                after(pe, "mxT_out", 4, s, 1)
                            xn2_transpose(s - 1, 0)
                        if u == 2:
                            if has(at, 1):
                                after(pe, "V_out", 4, s + 1, 2)
                            if has(at, 0):
                                residual_read()
                            else:
                                after(pe, "x2_out", 4, s - 1, 3)
                            logits(s - 1)
                        if u == 3:
                            if has(at, 1):
                                after(pe, "V_out", 4, s + 1, 3)
                            after(pe, "lg_out", 1, s - 1, 0)
                            if has(at, 0):
                                residual_read()
                            ranks(s - 1, 1 - par, at - 1)
                    if has(at, 0):
                        scores(s, par, u)
                    if has(at, -1) and u == 1:
                        after(pe, "xn2T_out", 2, s - 1, 0)
                        xn2_transpose(s - 1, 1)
                    if has(at1, 0):
                        residual_read()
                        if has(at, 1):
                            after(pe, "V_out", 4, s + 1, u)
                        if has(at, -1) and u == 2:
                            after(pe, "lg_out", 1, s - 1, 0)
                        if has(at, -1) and u == 3:
                            after(pe, "rk_out", 1, s - 1, 0)
                        project_out(q1, u1)

            slots(pe, step)

            def page_transpose(n, r):
                after(pe, "pn_out", 1, n, 0)
                bank = b4 if r % 2 == 0 else b5
                for c in range(2):
                    ins = pe.transpose(bank[:, c * P:(c + 1) * P], pn[:, r % PN, c * P:(c + 1) * P], ident)
                ins.then_inc(S["pT_done"], 1)

            def page_first(n, r):
                after(pe, "pT_out", 1, n, 0)
                bank = b6 if r % 2 == 0 else b7
                for i in range(2):
                    ins = pe.matmul(bank[0:HID, 0:P], w1p[:, r % PN, i * HID:(i + 1) * HID], pnT[:, r % 2, i * P:(i + 1) * P],
                                    start=(i == 0), stop=(i == 1))
                ins.then_inc(S["h_done"], 1)

            def page_second(n, r, first):
                after(pe, "h_out", 1, n, 0)
                if not first:
                    after(pe, "po_out", 1, n - 4, 0)
                pe.matmul(sc[r % 4][:, 0:D], hT[:, r % 2, :], w2p[:, r % PN, :], start=True, stop=True).then_inc(S["y_done"], 1)

            after(pe, "rk_out", 1, NQ - 1, 0)
            for n in range(PG):
                page_transpose(n, n)
                if n >= 1:
                    page_first(n - 1, n - 1)
                if n >= 2:
                    page_second(n - 2, n - 2, n - 2 < 4)
            with pe.Fori(1, PAGES // PG) as i:
                for r in range(PG):
                    page_transpose(i * PG + r, r)
                    page_first(i * PG + (r - 1), (r - 1) % PG)
                    page_second(i * PG + (r - 2), (r - 2) % PG, False)
            page_first(PAGES - 1, PG - 1)
            page_second(PAGES - 2, PG - 2, False)
            page_second(PAGES - 1, PG - 1, False)


def kernel(**inputs):
    import concourse.bacc as bacc
    from concourse.bass_utils import run_bass_kernel_spmd

    a = {k: np.asarray(v) for k, v in inputs.items()}
    x, c = a["x"], a["ctx_1024"]
    nb, t, d = x.shape

    def columns(w):
        return w.T.reshape(d // P, P, -1).transpose(1, 0, 2)

    def per_feature(v):
        return v.reshape(d // P, P).T

    def on_all(v):
        return np.broadcast_to(v, (P,) + v.shape)

    w1, w2 = a["L0_ffn_weights1"], a["L0_ffn_weights2"]
    e, _, hid = w1.shape
    b1 = np.concatenate([a["L0_ffn_bias1"].T, np.zeros((P - hid, e), np.float32)], 0)[:, :, None]
    arrays = {
        "x_in": x,
        "ctxT": c.reshape(nb // QB, QB, t, d // P, P).transpose(0, 4, 3, 1, 2).reshape(nb // QB, P, d // P, QB * t),
        "wq": columns(a["L0_xattn_Wq"]), "wk": columns(a["L0_xattn_Wk"]),
        "wv": columns(a["L0_xattn_Wv"]), "wo": columns(a["L0_xattn_Wo"]),
        "bq": per_feature(a["L0_xattn_bq"]), "bk": per_feature(a["L0_xattn_bk"]),
        "bv": on_all(a["L0_xattn_bv"]), "bo": on_all(a["L0_xattn_bo"]),
        "wr": columns(a["L0_ffn_router_w"]), "rb": on_all(a["L0_ffn_router_b"]),
        "w1": np.concatenate([w1.reshape(e, d // P, P, hid).transpose(2, 0, 1, 3).reshape(P, e, -1), b1], 2),
        "w2": np.concatenate([w2, a["L0_ffn_bias2"][:, None, :]], 1).transpose(1, 0, 2),
        "consts": constants(),
    }
    arrays = {k: np.ascontiguousarray(v) for k, v in arrays.items()}
    nc = bacc.Bacc("TRN2", target_bir_lowering=False, num_devices=1)
    args = [nc.dram_tensor(k, v.shape, mybir.dt.from_np(v.dtype), kind="ExternalInput").ap() for k, v in arrays.items()]
    args.append(nc.dram_tensor("out", x.shape, F32, kind="ExternalOutput").ap())
    build(nc, *args)
    r = run_bass_kernel_spmd(nc, [arrays], core_ids=[0])
    return r.results[0]["out"]
```

```python
from contextlib import ExitStack

import numpy as np

import concourse.bass as bass
from concourse import mybir

F32 = mybir.dt.float32
F32R = mybir.dt.float32r
BF16 = mybir.dt.bfloat16
I32 = mybir.dt.int32
U32 = mybir.dt.uint32
ALU = mybir.AluOpType
ACT = mybir.ActivationFunctionType
AX = mybir.AxisListType

P = 128
HD = 16
QB = 4
ROW = 260
COL_TOKEN, COL_EXPERT, COL_MEAN, COL_RSTD = 256, 257, 258, 259
NOWHERE = 1 << 30
EPS = 1e-5
PG = 16
PN = 8
GP = 4
LAG = 4
SCALE = HD ** -0.5
HI_LO = ((0, 0), (0, 1), (1, 0))
ROUND = 1.5 * 2.0 ** 23

C_IDENT, C_TRI, C_ONES, C_MASK, C_IOTA, C_TOKEN = 0, 128, 256, 320, 328, 360
C_ALL = 364


def constants():
    c = np.zeros((P, C_ALL), np.float32)
    p = np.arange(P)
    c[:, C_IDENT:C_IDENT + P] = np.eye(P)
    c[:, C_TRI:C_TRI + P] = p[:, None] < p[None, :]
    for m in range(2):
        c[:, C_ONES + 32 * m + 16 * m:C_ONES + 32 * m + 16 * m + 16] = 1.0
    c[:, C_MASK:C_MASK + 8] = p[:, None] // HD == np.arange(8)
    c[:, C_IOTA:C_IOTA + 32] = np.arange(32)
    c[:, C_TOKEN:C_TOKEN + QB] = p[:, None] + P * np.arange(QB)
    return c


def build(nc, x, ctxT, wq, wk, wv, wo, bq, bk, bv, bo, wr, rb, w1, w2, consts, out):
    NB = x.shape[0]
    D = x.shape[2]
    NQ = NB // QB
    E = wr.shape[2]
    HID = w2.shape[0] - 1
    TOKENS = NB * P
    PAGES = -(-(TOKENS // P + E) // PG) * PG
    x_q = x.rearrange("(q b) t d -> q t b d", b=QB)
    out_rows = out.rearrange("b t d -> (b t) d")
    pages = nc.dram_tensor("pages", (PAGES * P, ROW), F32).ap()
    page_view = pages.rearrange("(n p) c -> p n c", p=P)

    ctx = ExitStack()
    with ctx:
        def sb(name, shape, dt=F32):
            return ctx.enter_context(nc.sbuf_tensor(name, [P] + shape, dt))

        def ps(name):
            return ctx.enter_context(nc.psum_tensor(name, [P, 512], F32))

        def sem(name):
            return ctx.enter_context(nc.semaphore(name))

        cst = sb("cst", [C_ALL])
        wqkv = sb("wqkv", [3, 2, 2, D], F32R)
        wo_s = sb("wo_s", [2, D])
        wr_s = sb("wr_s", [2, P])
        bq_s, bk_s = sb("bq_s", [2]), sb("bk_s", [2])
        bq4 = sb("bq4", [2])
        bv_s, bo_s = sb("bv_s", [D]), sb("bo_s", [D])
        rb_s = sb("rb_s", [E])
        ident_b, tri_b, ones_b = sb("ident_b", [P], BF16), sb("tri_b", [P], BF16), sb("ones_b", [P], BF16)
        sel_b = sb("sel_b", [16, P], BF16)
        half = sb("half", [QB])
        xs = sb("xs", [2, QB, D])
        xb = sb("xb", [2, QB, D])
        work = sb("work", [PG * ROW])
        xn2T = work[:, 0:1024].rearrange("p (c t) -> p c t", c=2)
        xn2 = work[:, 1024:2048].rearrange("p (u d) -> p u d", u=QB)
        cT = work[:, 2048:3072].rearrange("p (c t) -> p c t", c=2)
        xn = work[:, 3072:3584].rearrange("p (v d) -> p v d", v=2)
        aT = work[:, 3584:4096].rearrange("p (a c t) -> p a c t", a=2, c=2)
        xnT = sb("xnT", [2, 2, QB * P], F32R)
        cHi, cLo = (sb(n, [2, 2, QB * P], F32R) for n in ("cHi", "cLo"))
        qT = sb("qT", [2, 2, 2, QB * P], F32R)
        kT = sb("kT", [2, 2, 2, QB * P], F32R)
        qM = sb("qM", [2, 2, 2, 8, P], F32R)
        kTh = kT[:, :, :, :, :].bitcast(BF16).rearrange("p a l c (t w) -> p a l c t w", w=2)[:, :, 0, :, :, 1]
        qMh = qM[:, :, :, :, :, :].bitcast(BF16).rearrange("p a l c h (t w) -> p a l c h t w", w=2)[:, :, 0, :, :, :, 1]
        pv = sb("pv", [2 * 2048 + 2 * QB * 512])
        vs = pv[:, 4096:8192].rearrange("p (a u g m d) -> p a u g m d", a=2, u=QB, g=8, m=4)
        mx = sb("mx", [2, P], BF16)
        mxT = sb("mxT", [2, P], BF16)
        pt = pv[:, 0:4096].rearrange("p (a j k) -> p a j k", a=2, j=4)
        wraw = pv[:, 0:6 * D].rearrange("p (w i d) -> p w i d", w=3, i=2)
        rz = sb("rz", [2 * P])
        row = sb("row", [2, QB, ROW])
        st1, ag1, rs1 = sb("st1", [QB, 6]), sb("ag1", [QB, 2]), sb("rs1", [QB])
        st2 = sb("st2", [QB, 6])
        lg = sb("lg", [QB, E])
        top, topi, idxf = sb("top", [QB, 8]), sb("topi", [QB, 8], U32), sb("idxf", [QB])
        hot = sb("hot", [2, QB, E], BF16)
        seen = sb("seen", [E], BF16)
        rk = sb("rk", [QB + 1, E])
        B = sb("B", [E])
        Doff = sb("Doff", [E])
        T0 = sb("T0", [1])
        fresh, run, noff, dd = sb("fresh", [E]), sb("run", [E]), sb("noff", [E]), sb("dd", [E])
        zer = sb("zer", [E])
        t1, t2 = sb("t1", [QB, E]), sb("t2", [QB, E])
        grew, shift = sb("grew", [E]), sb("shift", [E])
        slot = sb("slot", [QB])
        slot_i = sb("slot_i", [2, QB], U32)
        tok = sb("tok", [QB])
        tsum = sb("tsum", [E])
        empty = sb("empty", [ROW])
        rowf = row[:, :, :, :].rearrange("p a u c -> p (a u c)")
        table = rowf[0:1, 1600:1600 + PAGES].bitcast(I32)
        w1s = sb("w1s", [E, 2 * HID + 1])
        w1p = rowf[:, 0:PN * (2 * HID + 1)].rearrange("p (n c) -> p n c", n=PN)
        w2p = xs[0:HID + 1].rearrange("p a u d -> p (a u) d")
        w2s = pv[0:HID + 1, :].rearrange("p (e d) -> p e d", d=D)
        pr = work[:, :].rearrange("p (n c) -> p n c", c=ROW)
        pn = xb[:, :, :, :].rearrange("p a u d -> p (a u d)")[:, 0:PN * D].rearrange("p (n c) -> p n c", c=D)
        pnT = rowf[:, 1040:1040 + 4 * P].rearrange("p (n t) -> p n t", n=2)
        hT = rz[0:HID + 1].rearrange("p (n t) -> p n t", n=2)

        sc = [ps(f"sc{j}") for j in range(4)]
        b4, b5, b6, b7 = ps("b4"), ps("b5"), ps("b6"), ps("b7")
        b5h = b5[:, :].bitcast(BF16)

        names = """ld_w ld_w2 fill ld_x0 ld_x1 ld_c0 ld_c1 table_in page_in0 page_in1 page_in2 page_in3
          scattered wrote0 wrote1 wrote2 wrote3 ld_w1 ld_experts
          cst_ready pool_init dve_init
          S_done xnT_done proj_done V_done mxT_done PV_done T_done O_done xn2T_done lg_done rk_done
          xnT_out ctx_hi ctx_out hi_out lo_out xnTl_out mask_out w_hi exp_out xn2T_out
          max_out V_out lg_out mxT_out inv_out aT_out x2_out stat2_out agg2_out xn2_out
          stat1_out agg1_out xn_out top_out topi_out idx_out hot_out rk_out tsum_out seen_out
          need_out need_frac need_round pages_run pages_first fresh_start fresh_shift
          in_fresh old_slot fresh_step slot_each slot_own slot_sum page_total grew_out B_out shift_out D_out slot_out tok_next
          var2_out rstd2_out var1_out rstd1_out xb_out tok_out
          pn_out pT_done h_done y_done pT_out h_out po_out""".split()
        S = {n: sem(n) for n in names}

        def after(eng, name, per, q, k):
            eng.wait_ge(S[name], q * per + (k + 1))

        def apart(eng, *waits):
            waits = [(S[name], value if isinstance(value, int) else eng.to_reg(value)) for name, value in waits]
            eng.wait_ge(*settled[eng.engine])
            for semaphore, value in waits:
                eng.wait_ge(semaphore, value)

        def arrived(eng, name, q, par):
            eng.wait_ge(S[f"{name}{par}"], (q - par) * 8 + 16)

        ET = mybir.EngineType
        settled = {ET.DVE: (S["dve_init"], 4), ET.Pool: (S["pool_init"], 8), ET.SP: (S["pool_init"], 7)}

        block = ctx.enter_context(nc.Block())
        LO, HI = 2, NQ - 2

        def slots(eng, step):
            for s in range(LO):
                step(s, s % 2, s)
            with eng.Fori(0, (HI - LO) // 2) as i:
                for k in range(2):
                    step(i * 2 + (LO + k), k, LO)
            for s in range(HI, NQ + 2):
                step(s, s % 2, s)

        def has(at, lead):
            return 0 <= at + lead < NQ

        @block.sync
        def _(sp):
            sp.dma_start(xs[:, 0], x_q[0:1].rearrange("a t b d -> t (a b) d")).then_inc(S["ld_x0"], 16)
            for dst, src in ((cst[:, :], consts), (wraw[:, 0], wq), (wraw[:, 1], wk), (wraw[:, 2], wv),
                             (bq_s[:, :], bq), (bk_s[:, :], bk), (bv_s[:, :], bv)):
                sp.dma_start(dst, src).then_inc(S["ld_w"], 16)

            def load(q, par, at):
                if at >= 2:
                    apart(sp, ("xn_out", q * 4 - 4), ("xb_out", q - 1))
                if at >= 1:
                    sp.dma_start(xs[:, par], x_q[bass.ds(q, 1)].rearrange("a t b d -> t (a b) d")).then_inc(S[f"ld_x{par}"], 16)
                if at >= 1:
                    apart(sp, ("ctx_out", q))
                sp.dma_start(cT, ctxT[bass.ds(q, 1)].rearrange("a p c t -> p (a c) t")).then_inc(S[f"ld_c{par}"], 16)

            load(0, 0, 0)
            for dst, src in ((wo_s[:, :, :], wo), (bo_s[:, :], bo), (rb_s[:, :], rb)):
                sp.dma_start(dst, src).then_inc(S["ld_w2"], 16)
            sp.wait_ge(S["pool_init"], 7)
            sp.dma_start(wr_s[:, :, 0:E], wr).then_inc(S["ld_w2"], 16)
            load(1, 1, 1)
            sp.dma_start(w1s[:, :, :], w1).then_inc(S["ld_experts"], 16)
            with sp.Fori(0, (NQ - 2) // 2) as i:
                for k in range(2):
                    load(i * 2 + (2 + k), k, 2)

            sp.wait_ge(S["PV_done"], 4 * NQ)
            sp.dma_start(w2s, w2).then_inc(S["ld_experts"], 16)
            sp.wait_ge(S["scattered"], 64 * NQ)
            with nc.allow_non_contiguous_dma(reason="one word of each page"):
                sp.dma_start(table, pages.rearrange("(n p) c -> n p c", p=P)[:, 0, COL_EXPERT:COL_EXPERT + 1]
                             .rearrange("n c -> c n").bitcast(I32)).then_inc(S["table_in"], 16)

            def load_pages(n, r, first):
                if not first:
                    sp.wait_ge(S[f"wrote{r // GP}"], (n - r) * (16 * GP // PG))
                sp.dma_start(pr[:, r:r + GP, :], page_view[:, bass.ds(n, GP), :]).then_inc(S[f"page_in{r // GP}"], 16)

            for n in range(0, PG, GP):
                load_pages(n, n, True)
            with sp.Fori(1, PAGES // PG) as i:
                for r in range(0, PG, GP):
                    load_pages(i * PG + r, r, False)
            for g in range(PG // GP):
                sp.wait_ge(S[f"wrote{g}"], 16 * GP * (PAGES // PG))

        @block.gpsimd
        def _(pool):
            pool.memset(empty[:, :], 0.0).then_inc(S["pool_init"], 1)
            pool.memset(mx[:, :, :], 0.0).then_inc(S["pool_init"], 1)
            pool.memset(seen[:, :], 0.0).then_inc(S["pool_init"], 1)
            pool.memset(vs[:, 0, :, :, :, :], 0.0).then_inc(S["pool_init"], 1)
            pool.memset(vs[:, 1, :, :, :, :], 0.0).then_inc(S["pool_init"], 1)
            pool.memset(half[:, :], -0.5).then_inc(S["pool_init"], 1)
            pool.memset(wr_s[:, :, :], 0.0).then_inc(S["pool_init"], 1)
            pool.wait_ge(S["pool_init"], 7)
            pool.memset(empty[:, COL_TOKEN:COL_TOKEN + 1].bitcast(I32), NOWHERE).then_inc(S["pool_init"], 1)
            pool.wait_ge(S["pool_init"], 8)
            last_slot, last_token = pool.to_reg(PAGES * P - 1), pool.to_reg(TOKENS - 1)

            def rstd1(q):
                apart(pool, ("agg1_out", q * 4 + 4))
                pool.tensor_scalar(rs1[:, :], ag1[:, :, 1], EPS, None, ALU.add).then_inc(S["var1_out"], 1)
                after(pool, "var1_out", 1, q, 0)
                pool.tensor_tensor(rs1[:, :], rs1[:, :], half[:, :], ALU.pow).then_inc(S["rstd1_out"], 1)

            def rstd2(q, par):
                apart(pool, ("agg2_out", q * 4 + 4))
                v = row[:, par, :, COL_RSTD]
                pool.tensor_scalar(v, v, EPS, None, ALU.add).then_inc(S["var2_out"], 1)
                after(pool, "var2_out", 1, q, 0)
                pool.tensor_tensor(v, v, half[:, :], ALU.pow).then_inc(S["rstd2_out"], 1)

            def add_bo(q, par, at):
                if at == 0:
                    pool.wait_ge(S["ld_w2"], 64)
                arrived(pool, "ld_x", q, par)
                if at >= 2:
                    after(pool, "x2_out", 4, q - 2, 3)
                pool.tensor_tensor(xb[:, par], xs[:, par], bo_s[:, :].unsqueeze(1).to_broadcast([P, QB, D]),
                                   ALU.add).then_inc(S["xb_out"], 1)

            def split(q, par, at):
                used = [("proj_done", q * 4 - 4), ("V_done", q * 4 - 4)] if at >= 2 else []
                apart(pool, (f"ld_c{par}", (q - par) * 8 + 16), *used)
                pool.tensor_copy(cHi[:, par], cT).then_inc(S["ctx_hi"], 1)
                apart(pool, ("ctx_hi", q + 1))
                pool.tensor_tensor(cLo[:, par], cT, cHi[:, par].bitcast(F32), ALU.subtract).then_inc(S["ctx_out"], 1)

            def scatter(q, par, at):
                if at == 0:
                    pool.wait_ge(S["fill"], 16 * NF)
                apart(pool, ("slot_out", q + 1))
                for u in range(QB):
                    pool.indirect_dma_start(
                        pages, bass.IndirectOffsetOnAxis(slot_i[:, par, u:u + 1], 0), row[:, par, u, :], None,
                        bounds_check=last_slot, oob_is_err=False).then_inc(S["scattered"], 16)

            rstd1(0)
            split(0, 0, 0)
            rstd1(1)
            add_bo(0, 0, 0)
            split(1, 1, 1)
            NF = 8
            for f in range(NF):
                n = PAGES // NF
                pool.dma_start(page_view[:, n * f:n * (f + 1), :],
                               empty[:, :].unsqueeze(1).to_broadcast([P, n, ROW])).then_inc(S["fill"], 16)

            def step(s, par, at):
                if has(at, -2):
                    scatter(s - 2, par, at - 2)
                if has(at, -1):
                    rstd2(s - 1, 1 - par)
                if has(at, 2):
                    rstd1(s + 2)
                if has(at, 1):
                    add_bo(s + 1, 1 - par, at + 1)
                if has(at, 2):
                    split(s + 2, par, at + 2)

            slots(pool, step)

            def write_page(n, r):
                apart(pool, ("po_out", n + 1))
                pool.indirect_dma_start(
                    out_rows, bass.IndirectOffsetOnAxis(pr[:, r, COL_TOKEN:COL_TOKEN + 1].bitcast(U32), 0),
                    pr[:, r, 0:D], None, bounds_check=last_token, oob_is_err=False).then_inc(S[f"wrote{r // GP}"], 16)

            with pool.Fori(0, PAGES // PG) as i:
                for r in range(PG):
                    write_page(i * PG + r, r)

        @block.scalar
        def _(act):
            act.wait_ge(S["cst_ready"], 7)

            def xnT_copy(q, h, at):
                after(act, "xnT_done", 2, q, h)
                if at >= 1:
                    after(act, "proj_done", 4, q - 1, 1)
                src = b5[:, :].rearrange("p (u c t) -> p c u t", u=2, c=2)
                dst = xnT[:, 0, :, 2 * P * h:2 * P * (h + 1)].rearrange("p c (u t) -> p c u t", u=2)
                for c in range(2):
                    ins = act.activation(dst[:, c], src[:, c], ACT.Copy)
                ins.then_inc(S["xnT_out"], 1)

            def proj_hi(q, par, k, at):
                after(act, "proj_done", 4, q, k)
                if k < 2:
                    act.activation(qT[:, par, 0, k], b4[:, :], ACT.Identity, bias=bq4[:, k:k + 1]).then_inc(S["hi_out"], 1)
                else:
                    if at >= 2:
                        after(act, "T_done", 16, q - 2, 15)
                    act.activation(kT[:, par, 0, k - 2], b4[:, :], ACT.Identity, bias=bk_s[:, k - 2:k - 1]).then_inc(S["hi_out"], 1)

            def masks(q, par, u, at):
                if u == 0:
                    after(act, "hi_out", 4, q, 1)
                    after(act, "lo_out", 4, q, 1)
                if at >= 1 or u >= 2:
                    qq, uu = (q, u - 2) if u >= 2 else (q - 1, u + 2)
                    after(act, "T_done", 16, qq, 4 * uu + 3)
                for h in range(8):
                    ins = act.activation(qM[:, u % 2, :, :, h, :], qT[:, par, :, :, u * P:(u + 1) * P].bitcast(F32), ACT.Copy,
                                         scale=cst[:, C_MASK + h:C_MASK + h + 1])
                ins.then_inc(S["mask_out"], 1)

            def exps(q, u, at):
                for j in range(4):
                    after(act, "T_done", 16, q, 4 * u + j)
                    if j == 0 and (at >= 1 or u >= 2):
                        qq, uu = (q, u - 2) if u >= 2 else (q - 1, u + 2)
                        after(act, "PV_done", 4, qq, uu)
                    act.activation(pt[:, u % 2, j], sc[j][:, :], ACT.Exp).then_inc(S["exp_out"], 1)

            def xn2T_copy(q, h, at):
                after(act, "xn2T_done", 2, q, h)
                if at >= 1:
                    after(act, "lg_done", 1, q - 1, 0)
                src = b5[:, :].rearrange("p (u c t) -> p c u t", u=2, c=2)
                dst = xn2T[:, :, 2 * P * h:2 * P * (h + 1)].rearrange("p c (u t) -> p c u t", u=2)
                for c in range(2):
                    ins = act.activation(dst[:, c], src[:, c], ACT.Copy)
                ins.then_inc(S["xn2T_out"], 1)

            xnT_copy(0, 0, 0)
            xnT_copy(0, 1, 0)
            proj_hi(0, 0, 0, 0)
            proj_hi(0, 0, 1, 0)
            xnT_copy(1, 0, 1)
            xnT_copy(1, 1, 1)
            proj_hi(0, 0, 2, 0)
            proj_hi(0, 0, 3, 0)
            masks(0, 0, 0, 0)

            def step(s, par, at):
                for u in range(QB):
                    if has(at, 2) and u >= 2:
                        xnT_copy(s + 2, u - 2, at + 2)
                    if has(at, 1):
                        proj_hi(s + 1, 1 - par, u, at + 1)
                    if has(at, 0) and u < 3:
                        masks(s, par, u + 1, at)
                    if has(at, 1) and u == 3:
                        masks(s + 1, 1 - par, 0, at + 1)
                    if has(at, 0):
                        exps(s, u, at)
                    if has(at, -1) and u == 1:
                        xn2T_copy(s - 1, 0, at - 1)
                        xn2T_copy(s - 1, 1, at - 1)

            slots(act, step)

            def pnT_copy(n, r):
                after(act, "pT_done", 1, n, 0)
                act.activation(pnT[:, r % 2, :], b4[:, 0:256] if r % 2 == 0 else b5[:, 0:256], ACT.Copy).then_inc(S["pT_out"], 1)

            def h_copy(n, r, first):
                after(act, "h_done", 1, n, 0)
                if not first:
                    after(act, "y_done", 1, n - 2, 0)
                act.activation(hT[0:HID, r % 2, :], b6[0:HID, 0:P] if r % 2 == 0 else b7[0:HID, 0:P], ACT.Relu,
                               bias=w1p[0:HID, r % PN, 2 * HID:2 * HID + 1]).then_inc(S["h_out"], 1)

            for n in range(PG):
                pnT_copy(n, n)
                if n >= 1:
                    h_copy(n - 1, n - 1, n - 1 < 2)
            with act.Fori(1, PAGES // PG) as i:
                for r in range(PG):
                    pnT_copy(i * PG + r, r)
                    h_copy(i * PG + (r - 1), (r - 1) % PG, False)
            h_copy(PAGES - 1, PG - 1, False)

        @block.vector
        def _(dve):
            dve.memset(B[:, :], 0.0).then_inc(S["dve_init"], 1)
            dve.memset(Doff[:, :], 0.0).then_inc(S["dve_init"], 1)
            dve.memset(T0[:, :], 0.0).then_inc(S["dve_init"], 1)
            dve.memset(zer[:, :], 0.0).then_inc(S["dve_init"], 1)
            dve.wait_ge(S["dve_init"], 4)

            def stats1(q, par, batches=range(QB)):
                arrived(dve, "ld_x", q, par)
                for u in batches:
                    dve.bn_stats(st1[:, u, :], xs[:, par, u, :]).then_inc(S["stat1_out"], 1)
                for u in batches:
                    apart(dve, ("stat1_out", q * 4 + (u + 1)))
                    dve.bn_aggr(ag1[:, u, :], st1[:, u, :]).then_inc(S["agg1_out"], 1)

            def norm1(q, par, h, at):
                after(dve, "rstd1_out", 1, q, 0)
                if h == 1:
                    after(dve, "xnT_done", 2, q, 0)
                elif at >= 1:
                    after(dve, "xnT_done", 2, q - 1, 1)
                for v in range(2):
                    u = 2 * h + v
                    dve.tensor_scalar(xn[:, v, :], xs[:, par, u, :], ag1[:, u, 0:1], rs1[:, u:u + 1],
                                      ALU.subtract, ALU.mult).then_inc(S["xn_out"], 1)

            def maxima(q, u, at):
                if at >= 1 or u >= 2:
                    qq, uu = (q, u - 2) if u >= 2 else (q - 1, u + 2)
                    after(dve, "mxT_done", 4, qq, uu)
                after(dve, "S_done", 4, q, u)
                for j in range(4):
                    ins = dve.tensor_reduce(mx[:, u % 2, 4 * j:4 * j + 4], sc[j][:, :].rearrange("p (h k) -> p h k", h=4), AX.X, ALU.max)
                ins.then_inc(S["max_out"], 1)

            def v_copy(q, par, u, at):
                after(dve, "V_done", 4, q, u)
                if at >= 2:
                    after(dve, "PV_done", 4, q - 2, u)
                for m in range(2):
                    ins = dve.tensor_tensor(
                        vs[:, par, u, :, 3 * m, :], b6[:, 0:D].rearrange("p (g m d) -> p g m d", g=8, m=2)[:, :, m, :],
                        bv_s[:, :].rearrange("p (g m d) -> p g m d", g=8, m=2)[:, :, m, :], ALU.add)
                ins.then_inc(S["V_out"], 1)

            def xnT_lo(q, h):
                after(dve, "xnT_out", 2, q, h)
                src = b5[:, :].rearrange("p (u c t) -> p c u t", u=2, c=2)
                hi, lo = (xnT[:, l, :, 2 * P * h:2 * P * (h + 1)].rearrange("p c (u t) -> p c u t", u=2) for l in range(2))
                for c in range(2):
                    ins = dve.tensor_tensor(lo[:, c], src[:, c], hi[:, c].bitcast(F32), ALU.subtract)
                ins.then_inc(S["xnTl_out"], 1)

            def proj_lo(q, par, k, at):
                after(dve, "hi_out", 4, q, k)
                dst, bias = (qT, bq4) if k < 2 else (kT, bk_s)
                c = k % 2
                if at >= 2:
                    if k < 2:
                        after(dve, "mask_out", 4, q - 2, 3)
                    else:
                        after(dve, "T_done", 16, q - 2, 15)
                dve.scalar_tensor_tensor(dst[:, par, 1, c], b4[:, :], bias[:, c:c + 1], dst[:, par, 0, c].bitcast(F32),
                                         ALU.add, ALU.subtract).then_inc(S["lo_out"], 1)

            def mxT_copy(q, u, at):
                after(dve, "mxT_done", 4, q, u)
                dve.tensor_copy(mxT[:, u % 2, :], b5h[:, 0:P]).then_inc(S["mxT_out"], 1)

            def attend_copy(q, u, at):
                after(dve, "PV_done", 4, q, u)
                dve.reciprocal(rz[:, :], b7[:, 2 * P:4 * P]).then_inc(S["inv_out"], 1)
                after(dve, "inv_out", 4, q, u)
                if at >= 1 or u >= 2:
                    qq, uu = (q, u - 2) if u >= 2 else (q - 1, u + 2)
                    after(dve, "O_done", 4, qq, uu)
                dve.tensor_tensor(aT[:, u % 2].rearrange("p c t -> p (c t)"), b7[:, 0:2 * P], rz[:, :], ALU.mult).then_inc(S["aT_out"], 1)

            def residual(q, par, u, at):
                after(dve, "O_done", 4, q, u)
                after(dve, "xb_out", 1, q, 0)
                if at >= 2 and u == 0:
                    dve.wait_ge(S["scattered"], (q - 1) * 64)
                dve.tensor_tensor(row[:, par, u, 0:D], b6[:, D:2 * D], xb[:, par, u, :], ALU.add).then_inc(S["x2_out"], 1)
                after(dve, "x2_out", 4, q, u)
                dve.bn_stats(st2[:, u, :], row[:, par, u, 0:D]).then_inc(S["stat2_out"], 1)
                apart(dve, ("stat2_out", q * 4 + (u + 1)))
                dve.bn_aggr(row[:, par, u, COL_MEAN:COL_MEAN + 2], st2[:, u, :]).then_inc(S["agg2_out"], 1)

            def norm2(q, par, at):
                after(dve, "rstd2_out", 1, q, 0)
                if at >= 1:
                    after(dve, "xn2T_done", 2, q - 1, 1)
                for u in range(QB):
                    dve.tensor_scalar(xn2[:, u, :], row[:, par, u, 0:D], row[:, par, u, COL_MEAN:COL_MEAN + 1],
                                      row[:, par, u, COL_RSTD:COL_RSTD + 1], ALU.subtract, ALU.mult).then_inc(S["xn2_out"], 1)

            def logits(q):
                after(dve, "lg_done", 1, q, 0)
                dve.tensor_tensor(lg[:, :, :], b6[:, :].rearrange("p (u k) -> p u k", u=QB)[:, :, 0:E],
                                  rb_s[:, :].unsqueeze(1).to_broadcast([P, QB, E]), ALU.add).then_inc(S["lg_out"], 1)

            def choose(q):
                apart(dve, ("lg_out", q + 1))
                for u in range(QB):
                    dve.max(top[:, u, :], lg[:, u, :]).then_inc(S["top_out"], 1)
                for u in range(QB):
                    apart(dve, ("top_out", q * 4 + (u + 1)))
                    dve.max_index(topi[:, u, :], top[:, u, :], lg[:, u, :]).then_inc(S["topi_out"], 1)

            def one_hot(q, par, at):
                after(dve, "topi_out", 4, q, 3)
                dve.tensor_copy(idxf[:, :], topi[:, :, 0]).then_inc(S["idx_out"], 1)
                dve.tensor_copy(row[:, par, :, COL_EXPERT].bitcast(U32), topi[:, :, 0])
                dve.tensor_copy(row[:, par, :, COL_TOKEN].bitcast(I32), tok[:, :]).then_inc(S["tok_out"], 1)
                after(dve, "idx_out", 1, q, 0)
                dve.tensor_tensor(hot[:, par], cst[:, C_IOTA:C_IOTA + E].unsqueeze(1).to_broadcast([P, QB, E]),
                                  idxf[:, :].unsqueeze(2).to_broadcast([P, QB, E]), ALU.is_equal).then_inc(S["hot_out"], 1)
                after(dve, "tok_out", 1, q, 0)
                dve.tensor_scalar(tok[:, :], tok[:, :], float(QB * P), None, ALU.add).then_inc(S["tok_next"], 1)

            def rank_copy(q, par):
                after(dve, "rk_done", 1, q, 0)
                dve.tensor_copy(rk[:, :, :].rearrange("p u e -> p (u e)"), b6[:, 0:(QB + 1) * E]).then_inc(S["rk_out"], 1)
                after(dve, "hot_out", 1, q, 0)
                dve.tensor_reduce(tsum[:, :], hot[:, par].rearrange("p u e -> p e u"), AX.X, ALU.add).then_inc(S["tsum_out"], 1)
                after(dve, "tok_next", 1, q, 0)
                after(dve, "tsum_out", 1, q, 0)
                dve.tensor_tensor(seen[:, :], seen[:, :], tsum[:, :], ALU.add).then_inc(S["seen_out"], 1)
                after(dve, "seen_out", 1, q, 0)

            def own(name, q, ins):
                ins.then_inc(S[name], 1)
                after(dve, name, 1, q, 0)

            def each(t):
                return t[:, :].unsqueeze(1).to_broadcast([P, QB, E])

            def fresh_pages(q):
                after(dve, "rk_out", 1, q, 0)
                rank, count = rk[:, 0:QB, :], rk[:, QB, :]
                own("need_out", q, dve.tensor_tensor(fresh[:, :], count, B[:, :], ALU.subtract))
                dve.tensor_tensor(t1[:, :, :], rank, each(B), ALU.is_ge).then_inc(S["in_fresh"], 1)
                own("need_frac", q, dve.tensor_scalar(fresh[:, :], fresh[:, :], 1.0 / P, (P - 1.0) / (2 * P), ALU.mult, ALU.add))
                dve.tensor_tensor(t2[:, :, :], rank, each(Doff), ALU.add).then_inc(S["old_slot"], 1)
                own("need_round", q, dve.tensor_scalar(fresh[:, :], fresh[:, :], ROUND, ROUND, ALU.add, ALU.subtract))
                own("pages_run", q, dve.tensor_tensor_scan(run[:, :], fresh[:, :], zer[:, :], T0[:, 0:1], ALU.add, ALU.add))
                dve.tensor_copy(T0[:, 0:1], run[:, E - 1:E]).then_inc(S["page_total"], 1)
                own("pages_first", q, dve.tensor_tensor(noff[:, :], run[:, :], fresh[:, :], ALU.subtract))
                own("fresh_start", q, dve.scalar_tensor_tensor(noff[:, :], noff[:, :], float(P), B[:, :], ALU.mult, ALU.subtract))
                own("fresh_shift", q, dve.tensor_tensor(dd[:, :], noff[:, :], Doff[:, :], ALU.subtract))

            def place(q, par):
                after(dve, "in_fresh", 1, q, 0)
                own("fresh_step", q, dve.tensor_tensor(t1[:, :, :], t1[:, :, :], each(dd), ALU.mult))
                after(dve, "old_slot", 1, q, 0)
                own("slot_each", q, dve.tensor_tensor(t1[:, :, :], t1[:, :, :], t2[:, :, :], ALU.add))
                dve.tensor_scalar(grew[:, :], fresh[:, :], 1.0, None, ALU.min).then_inc(S["grew_out"], 1)
                dve.scalar_tensor_tensor(B[:, :], fresh[:, :], float(P), B[:, :], ALU.mult, ALU.add).then_inc(S["B_out"], 1)
                own("slot_own", q, dve.tensor_tensor(t1[:, :, :], t1[:, :, :], hot[:, par], ALU.mult))
                after(dve, "grew_out", 1, q, 0)
                dve.tensor_tensor(shift[:, :], grew[:, :], dd[:, :], ALU.mult).then_inc(S["shift_out"], 1)
                own("slot_sum", q, dve.tensor_reduce(slot[:, :], t1[:, :, :], AX.X, ALU.add))
                dve.tensor_copy(slot_i[:, par, :], slot[:, :]).then_inc(S["slot_out"], 1)
                after(dve, "shift_out", 1, q, 0)
                own("D_out", q, dve.tensor_tensor(Doff[:, :], Doff[:, :], shift[:, :], ALU.add))
                after(dve, "B_out", 1, q, 0)
                after(dve, "page_total", 1, q, 0)

            stats1(0, 0)
            dve.wait_ge(S["ld_w"], 16 * 7)
            dve.memset(ones_b[:, :], 1.0).then_inc(S["cst_ready"], 1)
            dve.tensor_copy(ident_b[:, :], cst[:, C_IDENT:C_IDENT + P]).then_inc(S["cst_ready"], 1)
            dve.tensor_copy(tri_b[:, :], cst[:, C_TRI:C_TRI + P]).then_inc(S["cst_ready"], 1)
            dve.tensor_scalar(sel_b[:, :, :], cst[:, C_IDENT:C_IDENT + 16].unsqueeze(2).to_broadcast([P, 16, P]), -1.0, None,
                              ALU.mult).then_inc(S["cst_ready"], 1)
            dve.tensor_scalar(bq4[:, :], bq_s[:, :], SCALE, None, ALU.mult).then_inc(S["cst_ready"], 1)
            for w in range(3):
                dve.tensor_scalar(wqkv[:, w, 0], wraw[:, w], SCALE if w == 0 else 1.0, None, ALU.mult).then_inc(S["w_hi"], 1)
            dve.wait_ge(S["w_hi"], 3)
            for w in range(3):
                ins = dve.scalar_tensor_tensor(wqkv[:, w, 1], wraw[:, w], SCALE if w == 0 else 1.0, wqkv[:, w, 0].bitcast(F32),
                                               ALU.mult, ALU.subtract)
            ins.then_inc(S["cst_ready"], 1)
            dve.tensor_copy(tok[:, :], cst[:, C_TOKEN:C_TOKEN + QB]).then_inc(S["cst_ready"], 1)
            dve.wait_ge(S["cst_ready"], 7)
            norm1(0, 0, 0, 0)
            norm1(0, 0, 1, 0)
            stats1(1, 1)
            xnT_lo(0, 0)
            xnT_lo(0, 1)
            norm1(1, 1, 0, 1)
            proj_lo(0, 0, 0, 0)
            proj_lo(0, 0, 1, 0)
            dve.wait_ge(S["pool_init"], 5)
            for u in range(QB):
                v_copy(0, 0, u, 0)
            norm1(1, 1, 1, 1)
            xnT_lo(1, 0)
            xnT_lo(1, 1)
            proj_lo(0, 0, 2, 0)
            proj_lo(0, 0, 3, 0)

            def step(s, par, at):
                for u in range(QB):
                    if has(at, 0):
                        maxima(s, u, at)
                    if has(at, 2) and u >= 2:
                        xnT_lo(s + 2, u - 2)
                    if has(at, 1):
                        v_copy(s + 1, 1 - par, u, at + 1)
                    if has(at, 1):
                        proj_lo(s + 1, 1 - par, u, at + 1)
                    if has(at, 2) and u in (0, 1):
                        stats1(s + 2, par, (2 * u, 2 * u + 1))
                    if has(at, -1) and u == 3:
                        one_hot(s - 1, 1 - par, at - 1)
                    if has(at, 0):
                        mxT_copy(s, u, at)
                    q1, par1, at1, u1 = (s, par, at, u - 1) if u else (s - 1, 1 - par, at - 1, 3)
                    if has(at1, 0):
                        attend_copy(q1, u1, at1)
                    if has(at, -1) and u == 1:
                        norm2(s - 1, 1 - par, at - 1)
                    if has(at, 2) and u in (1, 2):
                        norm1(s + 2, par, u - 1, at + 2)
                    if has(at, -1) and u == 2:
                        logits(s - 1)
                        choose(s - 1)
                    if has(at, -1) and u == 3:
                        rank_copy(s - 1, 1 - par)
                        fresh_pages(s - 1)
                    if has(at, -2) and u == 0:
                        place(s - 2, par)
                    if has(at1, 0):
                        residual(q1, par1, u1, at1)

            slots(dve, step)

            def page_norm(n, r):
                e = dve.value_load(table[0:1, bass.ds(n, 1)], min_val=0, max_val=E - 1)
                dve.tensor_copy(w1p[:, r % PN, :], w1s[:, bass.ds(e, 1), :].rearrange("p e h -> p (e h)"))
                dve.tensor_copy(w2p[:, r % PN, :], w2s[:, bass.ds(e, 1), :].rearrange("p e d -> p (e d)"))
                if r % GP == 0:
                    dve.wait_ge(S[f"page_in{r // GP}"], (n - r) * (16 // PG) + 16)
                dve.tensor_scalar(pn[:, r % PN, :], pr[:, r, 0:D], pr[:, r, COL_MEAN:COL_MEAN + 1],
                                  pr[:, r, COL_RSTD:COL_RSTD + 1], ALU.subtract, ALU.mult).then_inc(S["pn_out"], 1)

            def page_out(n, r):
                after(dve, "y_done", 1, n, 0)
                dve.scalar_tensor_tensor(pr[:, r, 0:D], sc[r % 4][:, 0:D], 0.0, pr[:, r, 0:D], ALU.max, ALU.add).then_inc(S["po_out"], 1)

            dve.wait_ge(S["table_in"], 16)
            dve.memset(hT[HID:HID + 1], 1.0)
            dve.wait_ge(S["ld_experts"], 32)
            for n in range(PG):
                page_norm(n, n)
                if n >= LAG:
                    page_out(n - LAG, n - LAG)
            with dve.Fori(1, PAGES // PG) as i:
                for r in range(PG):
                    page_norm(i * PG + r, r)
                    page_out(i * PG + (r - LAG), (r - LAG) % PG)
            for n in range(PAGES - LAG, PAGES):
                page_out(n, n % PG)

        @block.tensor
        def _(pe):
            ident = cst[:, C_IDENT:C_IDENT + P]
            pe.wait_ge(S["cst_ready"], 7)

            def xn_transpose(q, h, at):
                after(pe, "xn_out", 4, q, 2 * h + 1)
                for v in range(2):
                    for c in range(2):
                        ins = pe.transpose(b5[:, (2 * v + c) * P:(2 * v + c + 1) * P], xn[:, v, c * P:(c + 1) * P], ident)
                ins.then_inc(S["xnT_done"], 1)

            def xnT_read(q, h):
                after(pe, "xnT_out", 2, q, h)
                after(pe, "xnTl_out", 2, q, h)

            def project(q, par, k, at):
                c = k % 2
                if k == 0:
                    xnT_read(q, 1)
                if k == 2:
                    after(pe, "ctx_out", 1, q, 0)
                if k > 0:
                    after(pe, "lo_out", 4, q, k - 1)
                elif at >= 1:
                    after(pe, "lo_out", 4, q - 1, 3)
                for i in range(2):
                    for a, b in HI_LO:
                        src = xnT[:, b] if k < 2 else (cHi, cLo)[b][:, par]
                        ins = pe.matmul(b4[:, :], wqkv[:, k // 2, a, i, c * P:(c + 1) * P], src[:, i, :],
                                        start=(i == 0 and (a, b) == HI_LO[0]), stop=(i == 1 and (a, b) == HI_LO[-1]))
                ins.then_inc(S["proj_done"], 1)

            def values(q, par, u):
                if u == 0:
                    after(pe, "ctx_out", 1, q, 0)
                for i in range(2):
                    for a, b in HI_LO:
                        ins = pe.matmul(b6[:, 0:D], (cHi, cLo)[a][:, par, i, u * P:(u + 1) * P], wqkv[:, 2, b, i, :],
                                        start=(i == 0 and (a, b) == HI_LO[0]), stop=(i == 1 and (a, b) == HI_LO[-1]))
                ins.then_inc(S["V_done"], 1)

            def scores_for_max(q, par, u):
                after(pe, "mask_out", 4, q, u)
                if u == 0:
                    after(pe, "hi_out", 4, q, 3)
                for h in range(16):
                    ins = pe.matmul(sc[h // 4][:, h % 4 * P:(h % 4 + 1) * P], qMh[:, u % 2, h // 8, h % 8, :],
                                    kTh[:, par, h // 8, u * P:(u + 1) * P], start=True, stop=True)
                ins.then_inc(S["S_done"], 1)

            def max_transpose(q, u):
                after(pe, "max_out", 4, q, u)
                pe.transpose(b5h[:, 0:P], mx[:, u % 2, :], ident_b[:, :]).then_inc(S["mxT_done"], 1)

            def scores(q, par, u):
                if u == 0:
                    after(pe, "lo_out", 4, q, 3)
                for j in range(4):
                    c = j // 2
                    for a, b in HI_LO:
                        if (a, b) == HI_LO[-1]:
                            if j == 0:
                                after(pe, "mxT_out", 4, q, u)
                            for h in range(4):
                                pe.matmul(sc[j][:, h * P:(h + 1) * P], sel_b[:, 4 * j + h, :], mxT[:, u % 2, :],
                                          start=False, stop=False, skip_group_check=True)
                        ins = pe.matmul(sc[j][:, :], kT[:, par, a, c, u * P:(u + 1) * P],
                                        qM[:, u % 2, b, c, 4 * (j % 2):4 * (j % 2) + 4, :].rearrange("p h t -> p (h t)"),
                                        start=((a, b) == HI_LO[0]), stop=((a, b) == HI_LO[-1]))
                    ins.then_inc(S["T_done"], 1)

            def attend(q, par, u):
                for part in range(2):
                    for c in range(2):
                        for m in range(2):
                            for j in range(4):
                                h = 8 * c + 2 * j + m
                                w = (vs[:, par, u, 4 * c + j].rearrange("p a d -> p (a d)")[:, 32 * m:32 * m + 32] if part == 0
                                     else cst[:, C_ONES + 32 * m:C_ONES + 32 * m + 32])
                                ins = pe.matmul(b7[32 * j:32 * j + 32, (2 * part + c) * P:(2 * part + c + 1) * P], w,
                                                pt[:, u % 2, h // 4, h % 4 * P:(h % 4 + 1) * P], start=(m == 0), stop=(m == 1))
                ins.then_inc(S["PV_done"], 1)

            def project_out(q, u):
                after(pe, "aT_out", 4, q, u)
                for i in range(2):
                    ins = pe.matmul(b6[:, D:2 * D], aT[:, u % 2, i, :], wo_s[:, i, :], start=(i == 0), stop=(i == 1))
                ins.then_inc(S["O_done"], 1)

            def xn2_transpose(q, h):
                after(pe, "xn2_out", 4, q, 2 * h + 1)
                for v in range(2):
                    for c in range(2):
                        ins = pe.transpose(b5[:, (2 * v + c) * P:(2 * v + c + 1) * P], xn2[:, 2 * h + v, c * P:(c + 1) * P], ident)
                ins.then_inc(S["xn2T_done"], 1)

            def logits(q):
                after(pe, "xn2T_out", 2, q, 1)
                for u in range(QB):
                    for i in range(2):
                        ins = pe.matmul(b6[:, u * P:(u + 1) * P], xn2T[:, i, u * P:(u + 1) * P], wr_s[:, i, :],
                                        start=(i == 0), stop=(i == 1))
                ins.then_inc(S["lg_done"], 1)

            def ranks(q, par, at):
                after(pe, "hot_out", 1, q, 0)
                if at >= 1:
                    after(pe, "seen_out", 1, q - 1, 0)
                pe.matmul(b6[:, 0:QB * E], ones_b[:, :], seen[:, :].unsqueeze(1).to_broadcast([P, QB, E]), start=True, stop=False)
                for v in range(QB - 1):
                    pe.matmul(b6[:, (v + 1) * E:QB * E], ones_b[:, :], hot[:, par, v:v + 1].to_broadcast([P, QB - 1 - v, E]),
                              start=False, stop=False, skip_group_check=True)
                pe.matmul(b6[:, 0:QB * E], tri_b[:, :], hot[:, par], start=False, stop=True)
                pe.matmul(b6[:, QB * E:(QB + 1) * E], ones_b[:, :], seen[:, :], start=True, stop=False)
                for v in range(QB):
                    ins = pe.matmul(b6[:, QB * E:(QB + 1) * E], ones_b[:, :], hot[:, par, v], start=False, stop=(v == QB - 1))
                ins.then_inc(S["rk_done"], 1)

            xn_transpose(0, 0, 0)
            xnT_read(0, 0)
            xn_transpose(0, 1, 0)
            project(0, 0, 0, 0)
            project(0, 0, 1, 0)
            for u in range(QB):
                if u:
                    after(pe, "V_out", 4, 0, u - 1)
                values(0, 0, u)
            xn_transpose(1, 0, 1)
            xnT_read(1, 0)
            xn_transpose(1, 1, 1)
            project(0, 0, 2, 0)
            project(0, 0, 3, 0)
            pe.wait_ge(S["ld_w2"], 64)

            def step(s, par, at):
                for u in range(QB):
                    q1, par1, at1, u1 = (s, par, at, u - 1) if u else (s - 1, 1 - par, at - 1, 3)

                    def residual_read():
                        q2, u2 = (q1, u1 - 1) if u1 else (q1 - 1, 3)
                        if has(at1 if u1 else at1 - 1, 0):
                            after(pe, "x2_out", 4, q2, u2)

                    if has(at, 0):
                        if u == 0:
                            after(pe, "V_out", 4, s, 3)
                        if has(at1, 0):
                            after(pe, "exp_out", 16, q1, 4 * u1 + 3)
                        scores_for_max(s, par, u)
                    if has(at, 2) and u >= 2:
                        if has(at, -1) and u == 2:
                            after(pe, "xn2T_out", 2, s - 1, 1)
                        after(pe, "mxT_out", 4, q1, u1)
                        xn_transpose(s + 2, u - 2, at + 2)
                    if has(at, 1):
                        project(s + 1, 1 - par, u, at + 1)
                        if u > 0:
                            after(pe, "V_out", 4, s + 1, u - 1)
                        elif has(at, -2):
                            after(pe, "rk_out", 1, s - 2, 0)
                        if u == 3 and has(at, -1):
                            after(pe, "lg_out", 1, s - 1, 0)
                        residual_read()
                        values(s + 1, 1 - par, u)
                    if has(at1, 0):
                        after(pe, "exp_out", 16, q1, 4 * u1 + 3)
                        q2, u2 = (q1, u1 - 1) if u1 else (q1 - 1, 3)
                        if has(at1 if u1 else at1 - 1, 0):
                            after(pe, "aT_out", 4, q2, u2)
                        attend(q1, par1, u1)
                    if has(at, 0):
                        if has(at, 2) and u >= 2:
                            xnT_read(s + 2, u - 2)
                        elif has(at, -1) and u == 2:
                            after(pe, "xn2T_out", 2, s - 1, 1)
                        if at == 0 and u == 0:
                            xnT_read(1, 1)
                        max_transpose(s, u)
                    if has(at, -1):
                        if u == 2:
                            if has(at, 1):
                                after(pe, "V_out", 4, s + 1, 2)
                            if has(at, 0):
                                residual_read()
                            else:
                                after(pe, "x2_out", 4, s - 1, 3)
                            logits(s - 1)
                        if u == 3:
                            if has(at, 1):
                                after(pe, "V_out", 4, s + 1, 3)
                            after(pe, "lg_out", 1, s - 1, 0)
                            if has(at, 0):
                                residual_read()
                            ranks(s - 1, 1 - par, at - 1)
                    if has(at, 0):
                        scores(s, par, u)
                    if has(at, -1) and u == 1:
                        xn2_transpose(s - 1, 0)
                    if has(at1, 0):
                        residual_read()
                        if has(at, 1):
                            after(pe, "V_out", 4, s + 1, u)
                        if has(at, -1) and u == 2:
                            after(pe, "lg_out", 1, s - 1, 0)
                        if has(at, -1) and u == 3:
                            after(pe, "rk_out", 1, s - 1, 0)
                        project_out(q1, u1)
                    if has(at, -1) and u == 1:
                        after(pe, "xn2T_out", 2, s - 1, 0)
                        xn2_transpose(s - 1, 1)

            slots(pe, step)

            def page_transpose(n, r):
                after(pe, "pn_out", 1, n, 0)
                bank = b4 if r % 2 == 0 else b5
                for c in range(2):
                    ins = pe.transpose(bank[:, c * P:(c + 1) * P], pn[:, r % PN, c * P:(c + 1) * P], ident)
                ins.then_inc(S["pT_done"], 1)

            def page_first(n, r):
                after(pe, "pT_out", 1, n, 0)
                bank = b6 if r % 2 == 0 else b7
                for i in range(2):
                    ins = pe.matmul(bank[0:HID, 0:P], w1p[:, r % PN, i * HID:(i + 1) * HID], pnT[:, r % 2, i * P:(i + 1) * P],
                                    start=(i == 0), stop=(i == 1))
                ins.then_inc(S["h_done"], 1)

            def page_second(n, r, first):
                after(pe, "h_out", 1, n, 0)
                if not first:
                    after(pe, "po_out", 1, n - 4, 0)
                pe.matmul(sc[r % 4][:, 0:D], hT[:, r % 2, :], w2p[:, r % PN, :], start=True, stop=True).then_inc(S["y_done"], 1)

            after(pe, "rk_out", 1, NQ - 1, 0)
            for n in range(PG):
                page_transpose(n, n)
                if n >= 1:
                    page_first(n - 1, n - 1)
                if n >= 2:
                    page_second(n - 2, n - 2, n - 2 < 4)
            with pe.Fori(1, PAGES // PG) as i:
                for r in range(PG):
                    page_transpose(i * PG + r, r)
                    page_first(i * PG + (r - 1), (r - 1) % PG)
                    page_second(i * PG + (r - 2), (r - 2) % PG, False)
            page_first(PAGES - 1, PG - 1)
            page_second(PAGES - 2, PG - 2, False)
            page_second(PAGES - 1, PG - 1, False)


def kernel(**inputs):
    import concourse.bacc as bacc
    from concourse.bass_utils import run_bass_kernel_spmd

    a = {k: np.asarray(v) for k, v in inputs.items()}
    x, c = a["x"], a["ctx_1024"]
    nb, t, d = x.shape

    def columns(w):
        return w.T.reshape(d // P, P, -1).transpose(1, 0, 2)

    def per_feature(v):
        return v.reshape(d // P, P).T

    def on_all(v):
        return np.broadcast_to(v, (P,) + v.shape)

    w1, w2 = a["L0_ffn_weights1"], a["L0_ffn_weights2"]
    e, _, hid = w1.shape
    b1 = np.concatenate([a["L0_ffn_bias1"].T, np.zeros((P - hid, e), np.float32)], 0)[:, :, None]
    arrays = {
        "x_in": x,
        "ctxT": c.reshape(nb // QB, QB, t, d // P, P).transpose(0, 4, 3, 1, 2).reshape(nb // QB, P, d // P, QB * t),
        "wq": columns(a["L0_xattn_Wq"]), "wk": columns(a["L0_xattn_Wk"]),
        "wv": columns(a["L0_xattn_Wv"]), "wo": columns(a["L0_xattn_Wo"]),
        "bq": per_feature(a["L0_xattn_bq"]), "bk": per_feature(a["L0_xattn_bk"]),
        "bv": on_all(a["L0_xattn_bv"]), "bo": on_all(a["L0_xattn_bo"]),
        "wr": columns(a["L0_ffn_router_w"]), "rb": on_all(a["L0_ffn_router_b"]),
        "w1": np.concatenate([w1.reshape(e, d // P, P, hid).transpose(2, 0, 1, 3).reshape(P, e, -1), b1], 2),
        "w2": np.concatenate([w2, a["L0_ffn_bias2"][:, None, :]], 1).transpose(1, 0, 2),
        "consts": constants(),
    }
    arrays = {k: np.ascontiguousarray(v) for k, v in arrays.items()}
    nc = bacc.Bacc("TRN2", target_bir_lowering=False, num_devices=1)
    args = [nc.dram_tensor(k, v.shape, mybir.dt.from_np(v.dtype), kind="ExternalInput").ap() for k, v in arrays.items()]
    args.append(nc.dram_tensor("out", x.shape, F32, kind="ExternalOutput").ap())
    build(nc, *args)
    r = run_bass_kernel_spmd(nc, [arrays], core_ids=[0])
    return r.results[0]["out"]
```
